# Optimizing a Trainium2 kernel written in Bass

```python
import numpy as np
import jax
import jax.numpy as jnp

def _softmax(x, axis=-1):
    return jax.nn.softmax(x, axis=axis)

def _gelu(x):
    return jax.nn.gelu(x, approximate=True)

def _silu(x):
    return jax.nn.silu(x)

def _sigmoid(x):
    return jax.nn.sigmoid(x)

def _layernorm(x, axis=-1, eps=1e-05):
    m = jnp.mean(x, axis=axis, keepdims=True)
    v = jnp.var(x, axis=axis, keepdims=True)
    return (x - m) / jnp.sqrt(v + eps)

def _scatter_add(tgt, idx, src, axis=0):
    return tgt.at[idx].add(src)

def _segment_sum(src, seg, n):
    return jax.ops.segment_sum(src, seg, n)
kernel_name = 'mk_cond_seq_d4_seqx_r8_e497c7'

def setup_inputs(seed: int=0):
    np.random.seed(seed)
    _w = jnp.asarray

    def _rec_inputs():
        import jax
        import jax.numpy as jnp
        _rk = jax.random.key(seed)
        x = -0.0002928 + 1 * jax.random.normal(jax.random.fold_in(_rk, 1), (4, 256, 128), jnp.float32)
        _lenS = 256 - jax.random.randint(jax.random.fold_in(_rk, 7), (4,), 0, max(1, 256 // 4) + 1, jnp.int32)
        _lenS2 = 256 - jax.random.randint(jax.random.fold_in(_rk, 8), (4,), 0, max(1, 256 // 4) + 1, jnp.int32)
        cond_1024 = 0.0061147 + 1.02565 * jax.random.normal(jax.random.fold_in(_rk, 11), (4, 128), jnp.float32)
        _validS = jnp.arange(256)[None, :] < _lenS[:, None]
        _validS2 = jnp.arange(256)[None, :] < _lenS2[:, None]
        _causal = jnp.tril(jnp.ones((256, 256), dtype=bool))
        mask_BxSxSx11_ik0 = jnp.where(jnp.ones((4, 256, 256, 11), dtype=bool), 0, 1).astype(jnp.int32)
        return (x, cond_1024, mask_BxSxSx11_ik0)
    x, cond_1024, mask_BxSxSx11_ik0 = _rec_inputs()

    def _L0_cond_setup():
        import jax, jax.numpy as jnp
        import numpy as np
        B, T, DIM = (4, 128, 128)
        COND = 128
        HEADS, DH = (16, 64)
        INNER = HEADS * DH
        MLP = 512
        EPS = 1e-05

        def _layernorm(x):
            mu = jnp.mean(x, axis=-1, keepdims=True)
            var = jnp.mean(jnp.square(x - mu), axis=-1, keepdims=True)
            return (x - mu) * jax.lax.rsqrt(var + EPS)

        def _modulate(x, shift, scale):
            return x * (1.0 + scale) + shift

        def _attention(x, W_qkv, W_out, b_out):
            Bq, Tq, _ = x.shape
            qkv = x @ W_qkv
            q, k, v = jnp.split(qkv, 3, axis=-1)
            q = q.reshape(Bq, Tq, HEADS, DH)
            k = k.reshape(Bq, Tq, HEADS, DH)
            v = v.reshape(Bq, Tq, HEADS, DH)
            scale = DH ** (-0.5)
            attn = jnp.einsum('bqhd,bkhd->bhqk', q, k) * scale
            attn = jax.nn.softmax(attn, axis=-1)
            out = jnp.einsum('bhqk,bkhd->bqhd', attn, v).reshape(Bq, Tq, INNER)
            return out @ W_out + b_out

        def _ff(x, W1, b1, W2, b2):
            return jax.nn.gelu(x @ W1 + b1, approximate=False) @ W2 + b2
        key = jax.random.key(seed)
        ks = jax.random.split(key, 12)
        s = 0.02
        return {'x': jax.random.normal(ks[0], (B, T, DIM), jnp.float32), 'c': jax.random.normal(ks[1], (B, 1, COND), jnp.float32), 'W_mod': jax.random.normal(ks[2], (COND, 6 * DIM), jnp.float32) * s, 'b_mod': jax.random.normal(ks[3], (6 * DIM,), jnp.float32) * s, 'W_qkv': jax.random.normal(ks[4], (DIM, 3 * INNER), jnp.float32) * s, 'W_out': jax.random.normal(ks[5], (INNER, DIM), jnp.float32) * s, 'b_out': jax.random.normal(ks[6], (DIM,), jnp.float32) * s, 'W1': jax.random.normal(ks[7], (DIM, MLP), jnp.float32) * s, 'b1': jax.random.normal(ks[8], (MLP,), jnp.float32) * s, 'W2': jax.random.normal(ks[9], (MLP, DIM), jnp.float32) * s, 'b2': jax.random.normal(ks[10], (DIM,), jnp.float32) * s}
    _L0_cond_all = _L0_cond_setup()
    _L0_cond_in = {k: v for k, v in _L0_cond_all.items() if k in ('W_mod', 'b_mod', 'W_qkv', 'W_out', 'b_out', 'W1', 'b1', 'W2', 'b2')}
    del _L0_cond_all

    def _L1_cond_setup():
        import jax, jax.numpy as jnp
        import numpy as np
        NONGT = 20
        H = 16
        NEG = -9000000000000000.0

        def _gat_attention(self_feat, cond_adj, label_bias, Wq, bq, Wk, bk, Wout, bout):
            B, N, F = self_feat.shape
            ng = min(NONGT, N)
            dh = F // H
            kv = self_feat[:, :ng]
            qh = (self_feat @ Wq.T + bq).reshape(B, N, H, dh)
            kh = (kv @ Wk.T + bk).reshape(B, ng, H, dh)
            aff = jnp.einsum('bnhd,bmhd->bnhm', qh, kh) * (1.0 / np.sqrt(dh))
            mask = cond_adj[:, :, None, :] > 0
            aff = jnp.where(mask, aff, NEG) + label_bias[:, :, None, :]
            w = jax.nn.softmax(aff, axis=-1)
            out_t = jnp.einsum('bnhm,bmf->bnhf', w, kv)
            out = jnp.einsum('bnhf,hgf->bnhg', out_t, Wout) + bout.reshape(H, F // H)
            return out.reshape(B, N, F)

        def _forward(v, q, adj, W_self, b_self, w_bias, b_bias, Wq, bq, Wk, bk, Wout, bout):
            adj_f = adj.astype(jnp.float32)
            exp_v = v
            row_zero = exp_v.sum(-1) == 0
            q_exp = jnp.where(row_zero[..., None], 0.0, q[:, None, :])
            vcq = jnp.concatenate([exp_v, q_exp], axis=-1)
            self_feat = vcq @ W_self.T + b_self
            output = self_feat
            for d in range(2):
                A = adj_f if d == 0 else jnp.swapaxes(adj_f, 1, 2)
                A = A[:, :, :NONGT, :]
                cond = A.sum(-1)
                vb = A @ w_bias + b_bias
                output = output + _gat_attention(self_feat, cond, vb, Wq[d], bq[d], Wk[d], bk[d], Wout[d], bout[d])
            rel = jax.nn.relu(output)
            return exp_v + rel
        key = jax.random.key(seed)
        ks = jax.random.split(key, 8)
        B, N, L, F, Q = (32, 36, 11, 128, 128)
        IN = F + Q
        s = 0.02
        return {'v': jax.random.normal(ks[0], (B, N, F), jnp.float32), 'q': jax.random.normal(ks[1], (B, Q), jnp.float32), 'adj': jax.random.randint(ks[2], (B, N, N, L), 0, 2, jnp.int32), 'W_self': jax.random.normal(ks[3], (F, IN), jnp.float32) * s, 'b_self': jnp.zeros((F,), jnp.float32), 'w_bias': jax.random.normal(ks[4], (L,), jnp.float32) * s, 'b_bias': jnp.zeros((), jnp.float32), 'Wq': jax.random.normal(ks[5], (2, F, F), jnp.float32) * s, 'bq': jnp.zeros((2, F), jnp.float32), 'Wk': jax.random.normal(ks[6], (2, F, F), jnp.float32) * s, 'bk': jnp.zeros((2, F), jnp.float32), 'Wout': jax.random.normal(ks[7], (2, H, F // H, F), jnp.float32) * s, 'bout': jnp.zeros((2, F), jnp.float32)}
    _L1_cond_all = _L1_cond_setup()
    _L1_cond_in = {k: v for k, v in _L1_cond_all.items() if k in ('W_self', 'b_self', 'w_bias', 'b_bias', 'Wq', 'bq', 'Wk', 'bk', 'Wout', 'bout')}
    del _L1_cond_all

    def _L2_cond_setup():
        import jax, jax.numpy as jnp
        import numpy as np
        EPS = 1e-05

        def _sln(h, w, ln_g, ln_b, Wg, bg, Wb, bb):
            mu = jnp.mean(h, axis=-1, keepdims=True)
            var = jnp.mean((h - mu) ** 2, axis=-1, keepdims=True)
            ln = (h - mu) / jnp.sqrt(var + EPS) * ln_g + ln_b
            gamma = (w @ Wg.T + bg)[:, None, :]
            beta = (w @ Wb.T + bb)[:, None, :]
            return gamma * ln + beta
        key = jax.random.key(seed)
        ks = jax.random.split(key, 20)
        B, N, D = (4, 128, 128)
        F = 4 * D
        s = lambda fan: 1.0 / np.sqrt(fan)
        inp = {'hidden': jax.random.normal(ks[0], (B, N, D), jnp.float32), 'w': jax.random.normal(ks[1], (B, D), jnp.float32), 'ln_g': jnp.ones((D,), jnp.float32), 'ln_b': jnp.zeros((D,), jnp.float32), 'Wg': jax.random.normal(ks[2], (D, D), jnp.float32) * s(D), 'bg': jnp.zeros((D,), jnp.float32), 'Wb': jax.random.normal(ks[3], (D, D), jnp.float32) * s(D), 'bb': jnp.zeros((D,), jnp.float32), 'Wqkv': jax.random.normal(ks[4], (3 * D, D), jnp.float32) * s(D), 'bqkv': jnp.zeros((3 * D,), jnp.float32), 'Wp': jax.random.normal(ks[5], (D, D), jnp.float32) * s(D), 'bp': jnp.zeros((D,), jnp.float32), 'W1': jax.random.normal(ks[6], (F, D), jnp.float32) * s(D), 'b1': jnp.zeros((F,), jnp.float32), 'W2': jax.random.normal(ks[7], (D, F), jnp.float32) * s(F), 'b2': jnp.zeros((D,), jnp.float32), 'num_heads': 16}
        return inp
    _L2_cond_all = _L2_cond_setup()
    _L2_cond_in = {k: v for k, v in _L2_cond_all.items() if k in ('ln_g', 'ln_b', 'Wg', 'bg', 'Wb', 'bb', 'Wqkv', 'bqkv', 'Wp', 'bp', 'W1', 'b1', 'W2', 'b2')}
    del _L2_cond_all

    def _L3_cond_setup():
        import jax, jax.numpy as jnp
        import numpy as np
        D = 128
        H = 16
        HD = 4 * D
        B, T = (4, 128)
        EPS = 1e-05

        def _layernorm(x, g, b):
            mu = jnp.mean(x, axis=-1, keepdims=True)
            var = jnp.mean(jnp.square(x - mu), axis=-1, keepdims=True)
            return (x - mu) * jax.lax.rsqrt(var + EPS) * g + b

        def _attention(x, Wqkv, Wproj, bproj):
            b, t, c = x.shape
            hd = c // H
            qkv = (x @ Wqkv).reshape(b, t, 3, H, hd).transpose(2, 0, 3, 1, 4)
            q, k, v = (qkv[0], qkv[1], qkv[2])
            scale = hd ** (-0.5)
            scores = jnp.einsum('bhqd,bhkd->bhqk', q, k) * scale
            causal = jnp.tril(jnp.ones((t, t), bool))
            scores = jnp.where(causal, scores, -jnp.inf)
            attn = jax.nn.softmax(scores, axis=-1)
            out = jnp.einsum('bhqk,bhkd->bhqd', attn, v)
            out = out.transpose(0, 2, 1, 3).reshape(b, t, c)
            return out @ Wproj + bproj
        key = jax.random.key(seed)
        ks = jax.random.split(key, 12)
        s = 0.02
        return {'x': jax.random.normal(ks[0], (B, T, D), jnp.float32), 'condition': jax.random.normal(ks[1], (B, D), jnp.float32), 'Wqkv': jax.random.normal(ks[2], (D, 3 * D), jnp.float32) * s, 'Wproj': jax.random.normal(ks[3], (D, D), jnp.float32) * s, 'bproj': jnp.zeros((D,), jnp.float32), 'W1': jax.random.normal(ks[4], (D, HD), jnp.float32) * s, 'b1': jnp.zeros((HD,), jnp.float32), 'W2': jax.random.normal(ks[5], (HD, D), jnp.float32) * s, 'b2': jnp.zeros((D,), jnp.float32), 'g1': jnp.ones((D,), jnp.float32), 'be1': jnp.zeros((D,), jnp.float32), 'g2': jnp.ones((D,), jnp.float32), 'be2': jnp.zeros((D,), jnp.float32), 'Wada': jax.random.normal(ks[6], (D, 6 * D), jnp.float32) * s, 'bada': jax.random.normal(ks[7], (6 * D,), jnp.float32) * s}
    _L3_cond_all = _L3_cond_setup()
    _L3_cond_in = {k: v for k, v in _L3_cond_all.items() if k in ('Wqkv', 'Wproj', 'bproj', 'W1', 'b1', 'W2', 'b2', 'g1', 'be1', 'g2', 'be2', 'Wada', 'bada')}
    del _L3_cond_all
    return {'x': x, 'cond_1024': cond_1024, 'mask_BxSxSx11_ik0': mask_BxSxSx11_ik0, 'L0_cond_W_mod': _L0_cond_in['W_mod'], 'L0_cond_b_mod': _L0_cond_in['b_mod'], 'L0_cond_W_qkv': _L0_cond_in['W_qkv'], 'L0_cond_W_out': _L0_cond_in['W_out'], 'L0_cond_b_out': _L0_cond_in['b_out'], 'L0_cond_W1': _L0_cond_in['W1'], 'L0_cond_b1': _L0_cond_in['b1'], 'L0_cond_W2': _L0_cond_in['W2'], 'L0_cond_b2': _L0_cond_in['b2'], 'L1_cond_W_self': _L1_cond_in['W_self'], 'L1_cond_b_self': _L1_cond_in['b_self'], 'L1_cond_w_bias': _L1_cond_in['w_bias'], 'L1_cond_b_bias': _L1_cond_in['b_bias'], 'L1_cond_Wq': _L1_cond_in['Wq'], 'L1_cond_bq': _L1_cond_in['bq'], 'L1_cond_Wk': _L1_cond_in['Wk'], 'L1_cond_bk': _L1_cond_in['bk'], 'L1_cond_Wout': _L1_cond_in['Wout'], 'L1_cond_bout': _L1_cond_in['bout'], 'L2_cond_ln_g': _L2_cond_in['ln_g'], 'L2_cond_ln_b': _L2_cond_in['ln_b'], 'L2_cond_Wg': _L2_cond_in['Wg'], 'L2_cond_bg': _L2_cond_in['bg'], 'L2_cond_Wb': _L2_cond_in['Wb'], 'L2_cond_bb': _L2_cond_in['bb'], 'L2_cond_Wqkv': _L2_cond_in['Wqkv'], 'L2_cond_bqkv': _L2_cond_in['bqkv'], 'L2_cond_Wp': _L2_cond_in['Wp'], 'L2_cond_bp': _L2_cond_in['bp'], 'L2_cond_W1': _L2_cond_in['W1'], 'L2_cond_b1': _L2_cond_in['b1'], 'L2_cond_W2': _L2_cond_in['W2'], 'L2_cond_b2': _L2_cond_in['b2'], 'L3_cond_Wqkv': _L3_cond_in['Wqkv'], 'L3_cond_Wproj': _L3_cond_in['Wproj'], 'L3_cond_bproj': _L3_cond_in['bproj'], 'L3_cond_W1': _L3_cond_in['W1'], 'L3_cond_b1': _L3_cond_in['b1'], 'L3_cond_W2': _L3_cond_in['W2'], 'L3_cond_b2': _L3_cond_in['b2'], 'L3_cond_g1': _L3_cond_in['g1'], 'L3_cond_be1': _L3_cond_in['be1'], 'L3_cond_g2': _L3_cond_in['g2'], 'L3_cond_be2': _L3_cond_in['be2'], 'L3_cond_Wada': _L3_cond_in['Wada'], 'L3_cond_bada': _L3_cond_in['bada']}

def reference(x, cond_1024, mask_BxSxSx11_ik0, L0_cond_W_mod, L0_cond_b_mod, L0_cond_W_qkv, L0_cond_W_out, L0_cond_b_out, L0_cond_W1, L0_cond_b1, L0_cond_W2, L0_cond_b2, L1_cond_W_self, L1_cond_b_self, L1_cond_w_bias, L1_cond_b_bias, L1_cond_Wq, L1_cond_bq, L1_cond_Wk, L1_cond_bk, L1_cond_Wout, L1_cond_bout, L2_cond_ln_g, L2_cond_ln_b, L2_cond_Wg, L2_cond_bg, L2_cond_Wb, L2_cond_bb, L2_cond_Wqkv, L2_cond_bqkv, L2_cond_Wp, L2_cond_bp, L2_cond_W1, L2_cond_b1, L2_cond_W2, L2_cond_b2, L3_cond_Wqkv, L3_cond_Wproj, L3_cond_bproj, L3_cond_W1, L3_cond_b1, L3_cond_W2, L3_cond_b2, L3_cond_g1, L3_cond_be1, L3_cond_g2, L3_cond_be2, L3_cond_Wada, L3_cond_bada):
    import jax
    import jax.numpy as jnp

    def _L0_cond_ref(x, c, W_mod, b_mod, W_qkv, W_out, b_out, W1, b1, W2, b2):
        import jax, jax.numpy as jnp
        import numpy as np
        B, T, DIM = (4, 128, 128)
        COND = 128
        HEADS, DH = (16, 64)
        INNER = HEADS * DH
        MLP = 512
        EPS = 1e-05

        def _layernorm(x):
            mu = jnp.mean(x, axis=-1, keepdims=True)
            var = jnp.mean(jnp.square(x - mu), axis=-1, keepdims=True)
            return (x - mu) * jax.lax.rsqrt(var + EPS)

        def _modulate(x, shift, scale):
            return x * (1.0 + scale) + shift

        def _attention(x, W_qkv, W_out, b_out):
            Bq, Tq, _ = x.shape
            qkv = x @ W_qkv
            q, k, v = jnp.split(qkv, 3, axis=-1)
            q = q.reshape(Bq, Tq, HEADS, DH)
            k = k.reshape(Bq, Tq, HEADS, DH)
            v = v.reshape(Bq, Tq, HEADS, DH)
            scale = DH ** (-0.5)
            attn = jnp.einsum('bqhd,bkhd->bhqk', q, k) * scale
            attn = jax.nn.softmax(attn, axis=-1)
            out = jnp.einsum('bhqk,bkhd->bqhd', attn, v).reshape(Bq, Tq, INNER)
            return out @ W_out + b_out

        def _ff(x, W1, b1, W2, b2):
            return jax.nn.gelu(x @ W1 + b1, approximate=False) @ W2 + b2
        mod = jax.nn.silu(c) @ W_mod + b_mod
        sh_msa, sc_msa, g_msa, sh_mlp, sc_mlp, g_mlp = jnp.split(mod, 6, axis=-1)
        x = x + g_msa * _attention(_modulate(_layernorm(x), sh_msa, sc_msa), W_qkv, W_out, b_out)
        x = x + g_mlp * _ff(_modulate(_layernorm(x), sh_mlp, sc_mlp), W1, b1, W2, b2)
        return x

    def _L1_cond_ref(v, q, adj, W_self, b_self, w_bias, b_bias, Wq, bq, Wk, bk, Wout, bout):
        import jax, jax.numpy as jnp
        import numpy as np
        NONGT = 20
        H = 16
        NEG = -9000000000000000.0

        def _gat_attention(self_feat, cond_adj, label_bias, Wq, bq, Wk, bk, Wout, bout):
            B, N, F = self_feat.shape
            ng = min(NONGT, N)
            dh = F // H
            kv = self_feat[:, :ng]
            qh = (self_feat @ Wq.T + bq).reshape(B, N, H, dh)
            kh = (kv @ Wk.T + bk).reshape(B, ng, H, dh)
            aff = jnp.einsum('bnhd,bmhd->bnhm', qh, kh) * (1.0 / np.sqrt(dh))
            mask = cond_adj[:, :, None, :] > 0
            aff = jnp.where(mask, aff, NEG) + label_bias[:, :, None, :]
            w = jax.nn.softmax(aff, axis=-1)
            out_t = jnp.einsum('bnhm,bmf->bnhf', w, kv)
            out = jnp.einsum('bnhf,hgf->bnhg', out_t, Wout) + bout.reshape(H, F // H)
            return out.reshape(B, N, F)

        def _forward(v, q, adj, W_self, b_self, w_bias, b_bias, Wq, bq, Wk, bk, Wout, bout):
            adj_f = adj.astype(jnp.float32)
            exp_v = v
            row_zero = exp_v.sum(-1) == 0
            q_exp = jnp.where(row_zero[..., None], 0.0, q[:, None, :])
            vcq = jnp.concatenate([exp_v, q_exp], axis=-1)
            self_feat = vcq @ W_self.T + b_self
            output = self_feat
            for d in range(2):
                A = adj_f if d == 0 else jnp.swapaxes(adj_f, 1, 2)
                A = A[:, :, :NONGT, :]
                cond = A.sum(-1)
                vb = A @ w_bias + b_bias
                output = output + _gat_attention(self_feat, cond, vb, Wq[d], bq[d], Wk[d], bk[d], Wout[d], bout[d])
            rel = jax.nn.relu(output)
            return exp_v + rel
        return _forward(v, q, adj, W_self, b_self, w_bias, b_bias, Wq, bq, Wk, bk, Wout, bout)

    def _L2_cond_ref(hidden, w, ln_g, ln_b, Wg, bg, Wb, bb, Wqkv, bqkv, Wp, bp, W1, b1, W2, b2, num_heads):
        import jax, jax.numpy as jnp
        import numpy as np
        EPS = 1e-05

        def _sln(h, w, ln_g, ln_b, Wg, bg, Wb, bb):
            mu = jnp.mean(h, axis=-1, keepdims=True)
            var = jnp.mean((h - mu) ** 2, axis=-1, keepdims=True)
            ln = (h - mu) / jnp.sqrt(var + EPS) * ln_g + ln_b
            gamma = (w @ Wg.T + bg)[:, None, :]
            beta = (w @ Wb.T + bb)[:, None, :]
            return gamma * ln + beta
        B, N, D = hidden.shape
        hd = D // num_heads
        h = _sln(hidden, w, ln_g, ln_b, Wg, bg, Wb, bb)
        qkv = (h @ Wqkv.T + bqkv).reshape(B, N, num_heads, hd, 3)
        q = jnp.moveaxis(qkv[..., 0], 2, 1)
        k = jnp.moveaxis(qkv[..., 1], 2, 1)
        v = jnp.moveaxis(qkv[..., 2], 2, 1)
        energy = jnp.einsum('bhqd,bhkd->bhqk', q, k)
        att = jax.nn.softmax(energy, axis=-1) / D ** 0.5
        out = jnp.einsum('bhqk,bhkd->bhqd', att, v)
        out = jnp.moveaxis(out, 1, 2).reshape(B, N, D)
        out = out @ Wp.T + bp
        h1 = out + hidden
        h2 = _sln(h1, w, ln_g, ln_b, Wg, bg, Wb, bb)
        return h2 + h1

    def _L3_cond_ref(x, condition, Wqkv, Wproj, bproj, W1, b1, W2, b2, g1, be1, g2, be2, Wada, bada):
        import jax, jax.numpy as jnp
        import numpy as np
        D = 128
        H = 16
        HD = 4 * D
        B, T = (4, 128)
        EPS = 1e-05

        def _layernorm(x, g, b):
            mu = jnp.mean(x, axis=-1, keepdims=True)
            var = jnp.mean(jnp.square(x - mu), axis=-1, keepdims=True)
            return (x - mu) * jax.lax.rsqrt(var + EPS) * g + b

        def _attention(x, Wqkv, Wproj, bproj):
            b, t, c = x.shape
            hd = c // H
            qkv = (x @ Wqkv).reshape(b, t, 3, H, hd).transpose(2, 0, 3, 1, 4)
            q, k, v = (qkv[0], qkv[1], qkv[2])
            scale = hd ** (-0.5)
            scores = jnp.einsum('bhqd,bhkd->bhqk', q, k) * scale
            causal = jnp.tril(jnp.ones((t, t), bool))
            scores = jnp.where(causal, scores, -jnp.inf)
            attn = jax.nn.softmax(scores, axis=-1)
            out = jnp.einsum('bhqk,bhkd->bhqd', attn, v)
            out = out.transpose(0, 2, 1, 3).reshape(b, t, c)
            return out @ Wproj + bproj
        mod = jax.nn.silu(condition) @ Wada + bada
        sh_a, sc_a, gt_a, sh_m, sc_m, gt_m = jnp.split(mod, 6, axis=1)
        xn = _layernorm(x, g1, be1)
        xm = xn * (1.0 + sc_a[:, None, :]) + sh_a[:, None, :]
        x = x + gt_a[:, None, :] * _attention(xm, Wqkv, Wproj, bproj)
        xn = _layernorm(x, g2, be2)
        xm = xn * (1.0 + sc_m[:, None, :]) + sh_m[:, None, :]
        h = jax.nn.gelu(xm @ W1 + b1, approximate=False)
        x = x + gt_m[:, None, :] * (h @ W2 + b2)
        return x
    x = _L0_cond_ref(x, cond_1024[:, None, :], L0_cond_W_mod, L0_cond_b_mod, L0_cond_W_qkv, L0_cond_W_out, L0_cond_b_out, L0_cond_W1, L0_cond_b1, L0_cond_W2, L0_cond_b2)
    x = _L1_cond_ref(x, cond_1024, mask_BxSxSx11_ik0, L1_cond_W_self, L1_cond_b_self, L1_cond_w_bias, L1_cond_b_bias, L1_cond_Wq, L1_cond_bq, L1_cond_Wk, L1_cond_bk, L1_cond_Wout, L1_cond_bout)
    x = _L2_cond_ref(x, cond_1024, L2_cond_ln_g, L2_cond_ln_b, L2_cond_Wg, L2_cond_bg, L2_cond_Wb, L2_cond_bb, L2_cond_Wqkv, L2_cond_bqkv, L2_cond_Wp, L2_cond_bp, L2_cond_W1, L2_cond_b1, L2_cond_W2, L2_cond_b2, 16)
    x = _L3_cond_ref(x, cond_1024, L3_cond_Wqkv, L3_cond_Wproj, L3_cond_bproj, L3_cond_W1, L3_cond_b1, L3_cond_W2, L3_cond_b2, L3_cond_g1, L3_cond_be1, L3_cond_g2, L3_cond_be2, L3_cond_Wada, L3_cond_bada)
    return x

_drawn_inputs = setup_inputs


def setup_inputs(seed=0):
    import zlib

    import numpy as np

    out = dict(_drawn_inputs(seed))
    spreads = {'L1_cond_b_self': (0.0, 0.8),
     'L1_cond_bq': (0.0, 0.1),
     'L1_cond_bk': (0.0, 0.1),
     'L1_cond_bout': (0.0, 0.8),
     'L2_cond_ln_g': (1.0, 0.6),
     'L2_cond_ln_b': (0.0, 0.8),
     'L2_cond_bg': (0.0, 0.8),
     'L2_cond_bb': (0.0, 0.8),
     'L2_cond_bqkv': (0.0, 2.0),
     'L2_cond_bp': (0.0, 0.8),
     'L2_cond_b1': (0.0, 0.1),
     'L2_cond_b2': (0.0, 0.1),
     'L3_cond_bproj': (0.0, 2.0),
     'L3_cond_b1': (0.0, 0.8),
     'L3_cond_b2': (0.0, 2.0),
     'L3_cond_g1': (1.0, 0.6),
     'L3_cond_be1': (0.0, 0.8),
     'L3_cond_g2': (1.0, 0.6),
     'L3_cond_be2': (0.0, 0.8)}
    factors = {'L0_cond_W_mod': 7.571,
     'L0_cond_b_mod': 8.0,
     'L0_cond_W_qkv': 8.0,
     'L0_cond_W_out': 8.0,
     'L0_cond_b_out': 53.811,
     'L0_cond_W1': 8.0,
     'L0_cond_b1': 22.878,
     'L0_cond_W2': 8.0,
     'L0_cond_b2': 53.671,
     'L3_cond_Wqkv': 8.0,
     'L3_cond_Wproj': 8.0,
     'L3_cond_W1': 8.0,
     'L3_cond_W2': 8.0,
     'L3_cond_Wada': 4.28,
     'L3_cond_bada': 8.0,
     'L2_cond_Wqkv': 8.0,
     'L2_cond_Wp': 8.0}
    for name, (base, spread) in spreads.items():
        noise = np.random.default_rng([zlib.crc32(name.encode()), seed]).standard_normal(out[name].shape)
        drawn = base * np.exp(spread * noise) if base else spread * noise
        out[name] = jnp.asarray(drawn.astype(out[name].dtype))
    for name, factor in factors.items():
        out[name] = (out[name] * factor).astype(out[name].dtype)
    return out
```

```python
import math
from contextlib import ExitStack

import concourse.bass as bass
from concourse import mybir

ALU = mybir.AluOpType
ACT = mybir.ActivationFunctionType
AX_X = mybir.AxisListType.X
F32 = mybir.dt.float32
BF16 = mybir.dt.bfloat16
I32 = mybir.dt.int32

B, T, D = 4, 256, 128
PB = 2
NT = T // 128
TOK = PB * T
TILES = PB * NT
H = 16
DH0 = 64
DH = D // H
FF = 512
FC = FF // 128
NG, NL = 20, 11
NEG = -9000000000000000.0
MASKED = -1.0e30
EPS = 1e-5

W0_COLS = dict(mod=6 * D, v=H * DH0, out=8 * D, w1=FF, w2=FF)
W1_COLS = dict(self_v=D, self_q=D, q=2 * D, k=2 * D, out=2 * D)
W2_COLS = dict(gamma=D, beta=D, q=D, k=D, v=D)
W3_COLS = dict(q=D, k=D, v=D, w1=FF, w2=FF, ada=6 * D)
VEC_COLS = dict(mods=14, b_out0=1, b2_0=1, b1_0=4, b_self=1, bq1=2, bk1=2, bout1=2,
                ln_g=1, ln_b=1, bq2=1, bk2=1, bp=1, bproj=1, b2_3=1, b1_3=4, g1=1, be1=1, g2=1, be2=1, cond=4)


def columns(widths):
    at, out = 0, {}
    for name, n in widths.items():
        out[name] = (at, at + n)
        at += n
    return out, at


W0_AT, W0_N = columns(W0_COLS)
W1_AT, W1_N = columns(W1_COLS)
W2_AT, W2_N = columns(W2_COLS)
W3_AT, W3_N = columns(W3_COLS)
VEC_AT, VEC_N = columns(VEC_COLS)

(SC0A, SH0A, G0A, GB0A, SC0B, SH0B, G0B, GB0B, SC2, SH2, G2, GB2,
 SC3A, SH3A, G3A, GB3A, SC3B, SH3B, G3B, GB3B) = range(20)
MODS = 20

UNITS = PB * H
GH = 8
GROUPS = UNITS // GH
ST_LAG = GH + 3
PV_LAG = ST_LAG + 2
O_LAG = PV_LAG + 1
PT_RING = 3
EXP_LN_SET = "natural_log_exp_and_others"
PARTS = 3
SLOTS = PARTS * PARTS

LAYERS = (0, 2, 3)
LN_ORDER = ("0a", "0b", "2a", "2b", "3a", "3b")


def l1_steps():
    return range(TILES * 2 + 5)


def work_plan():
    plan = []

    def norm(name):
        plan.extend([("tok", name), ("fm", name)])

    def attention(layer):
        plan.extend(("mT", layer, g) for g in range(GROUPS))
        plan.append(("proj", layer))

    def mlp(layer):
        plan.extend(("ff", layer, c) for c in range(FC))
        plan.append(("y", layer))

    norm("0a")
    plan.extend(("G", h) for h in range(H))
    plan.extend(("V", t, n) for t in range(TILES) for n in range(2))
    attention(0)
    norm("0b")
    mlp(0)
    plan.extend(["nz", "sf", ("q1", 0), ("q1", 1), "k1", "v1"])
    for i in l1_steps():
        if i < 2 * TILES:
            plan.append(("s1", i))
        if 0 <= i - 4 < 2 * TILES:
            plan.append(("wT", i - 4))
    for layer in (2, 3):
        norm(f"{layer}a")
        plan.extend([("q", layer), ("k", layer), ("v", layer)])
        attention(layer)
        norm(f"{layer}b")
    mlp(3)
    return {key: n for n, key in enumerate(plan)}


WORK = work_plan()


def cond_seq_kernel(nc, x_t, adj, w0, wqk0, w1, w2, w3, wp2, wproj3, vecs, rows, out_t):
    with ExitStack() as ctx:
        def sb(name, shape, dt=F32):
            return ctx.enter_context(nc.sbuf_tensor(name, shape, dt))

        def sem(name):
            return ctx.enter_context(nc.semaphore(name))

        w0s = sb("w0s", [128, W0_N])
        w1s = sb("w1s", [128, W1_N])
        w2s = sb("w2s", [128, W2_N])
        w3s = sb("w3s", [128, W3_N])
        wpad = {2: sb("wp2s", [128, 4, D]), 3: sb("wproj3s", [128, 4, D])}
        vec = sb("vec", [128, VEC_N])
        bv2 = sb("bv2", [128, D])
        wbias = sb("wbias", [128, NL + 1])
        a0 = sb("a0", [128, H, D])
        ident = sb("ident", [128, 128])
        identb = sb("identb", [128, 128], BF16)
        ones = sb("ones", [128, 64])
        eps = sb("eps", [128, 1])
        lnd = sb("lnd", [128, 1])
        zero = sb("zero", [128, 1])
        sel = sb("sel", [128, GH, 128], BF16)
        mask_qk = sb("mask_qk", [128, 128], BF16)
        mask_kq = sb("mask_kq", [128, 128], BF16)
        mask1 = sb("mask1", [128, H, NG])
        mask2 = sb("mask2", [128, 4, D])
        silu = sb("silu", [128, 3, B])
        raw = sb("raw", [128, 14, B])
        mods_all = sb("mods_all", [128, MODS, B])
        qw_all = sb("qw_all", [1, B, D])
        bq1s = sb("bq1s", [128, 2])
        bout1 = sb("bout1", [128, 1])

        mods = sb("mods", [128, MODS, PB])
        qw = sb("qw", [1, PB, D])
        xT = sb("xT", [128, TOK])
        xb = sb("xb", [128, TOK])
        hT = sb("hT", [128, TOK])
        stats = sb("stats", [128, TILES, 6])
        mv = sb("mv", [128, TILES, 2])
        lnv = sb("lnv", [128, TILES])
        rstd = sb("rstd", [128, TILES])
        xn = sb("xn", [128, TILES, 128])
        big = sb("big", [128, H * TOK])
        gT = big[:, :].rearrange("p (h t) -> p h t", h=H)
        stacks = big[:, :].bitcast(BF16).rearrange("p (s h t) -> p s h t", s=2, h=H)
        room = sb("room", [128, TILES * H * DH0])
        wqk0s = room[0:DH0, :].rearrange("p (s h n) -> p s h n", s=2, h=H)
        hTb = sb("hTb", [128, TOK], BF16)
        room3 = sb("room3", [128, H * TOK // 2])
        gTb = room3[:, :].bitcast(BF16).rearrange("p (h t) -> p h t", h=H)
        parts = room3[:, 0:3 * TOK].bitcast(BF16).rearrange("p (s n t) -> p s n t", s=2, n=PARTS)
        rest = room3[:, 3 * TOK:5 * TOK].rearrange("p (s t) -> p s t", s=2)
        pairsum = sb("pairsum", [128, 2, T])
        v0 = room[:, :].rearrange("p (t n) -> p t n", t=TILES)
        ff = room[:, 0:FC * TOK].rearrange("p (c t) -> p c t", c=FC)
        vpad = sb("vpad", [128, TILES, H, 32])
        room2 = sb("room2", [128, 8 * TOK])
        oT = room2[:, :].rearrange("p (c t) -> p c t", c=8)
        vbd = room2[:, 0:8 * TOK // 2].rearrange("p (d b n) -> p d b n", d=2, b=PB)
        wT = room2[:, 4 * TOK:6 * TOK].rearrange("p (s n) -> p s n", s=2)
        q1T = room2[:, 6 * TOK:8 * TOK].rearrange("p (d t) -> p d t", d=2)
        negm = sb("negm", [128, 2, NT, GH])
        m2 = sb("m2", [128, 2, NT, 128], BF16)
        mT = sb("mT", [128, 2, T], BF16)
        pt = sb("pt", [128, PT_RING, NT * T])
        rden = sb("rden", [128, 2, T])
        adj_s = sb("adj_s", [128, 2, TILES, NG * NL], I32)
        adj_w = sb("adj_w", [128, 2, TILES * NG, NL])
        cond1 = sb("cond1", [128, 2, TILES * NG])
        vb1 = sb("vb1", [128, 2, TILES * NG])
        keep1 = sb("keep1", [128, 2, TILES * NG])
        bias1 = sb("bias1", [128, 2, TILES * NG])
        nz = sb("nz", [1, TOK])
        sfT = sb("sfT", [128, TOK])
        sfb = sb("sfb", [128, TOK])
        sfrep = sb("sfrep", [128, PB, 4, 32])
        kbd = sb("kbd", [128, 2, PB, H * NG])
        aff = sb("aff", [128, 4, H, NG])
        amax = sb("amax", [128, 4, H])
        asum = sb("asum", [128, 4, H])
        arec = sb("arec", [128, 4, H])
        wgt = sb("wgt", [128, 2, H, 32])

        psum = ctx.enter_context(nc.psum_tensor("psum", [128, 8, 512], F32))
        S_BANK, ST_BANK, O_BANK, W_BANK = 0, 2, 4, 6
        scratch = nc.dram_tensor("scratch", [2, PARTS, D, TOK], BF16).ap()

        weights_in = sem("weights_in")
        pads_zero = sem("pads_zero")
        consts = sem("consts")
        consts_step = sem("consts_step")
        act_exp_c = sem("act_exp_c")
        silu_ready = sem("silu_ready")
        setup_step = sem("setup_step")
        mods_full = sem("mods_full")
        qw_full = sem("qw_full")
        a0_full = sem("a0_full")
        a0_free = sem("a0_free")
        vcopy = sem("vcopy")

        def col(at, name, i=0, n=1):
            return vec[:, VEC_AT[name][0] + i:VEC_AT[name][0] + i + n]

        with nc.Block() as block:
            @block.sync
            def _(sp):
                sp.dma_start(vec[:], vecs).then_inc(weights_in, 16)
                sp.dma_start(w0s[:], w0).then_inc(weights_in, 16)
                sp.dma_start(wqk0s, wqk0).then_inc(weights_in, 16)
                sp.dma_start(w1s[:], w1).then_inc(weights_in, 16)
                sp.dma_start(w2s[:], w2).then_inc(weights_in, 16)
                sp.dma_start(w3s[:], w3).then_inc(weights_in, 16)
                sp.dma_start(bv2[:], rows[0:1, 0:D].broadcast_to([128, D])).then_inc(weights_in, 16)
                sp.dma_start(wbias[:], rows[0:1, D:D + NL + 1].broadcast_to([128, NL + 1])).then_inc(weights_in, 16)
                sp.wait_ge(pads_zero, 2)
                for src, dst in ((wp2, wpad[2]), (wproj3, wpad[3])):
                    by_j = src.rearrange("(g j d) n -> j d g n", g=4, j=4)
                    for j in range(4):
                        sp.dma_start(dst[32 * j:32 * j + DH, :, :], by_j[j]).then_inc(weights_in, 16)
                sp.wait_ge(weights_in, 16 * 16)

            @block.gpsimd
            def _(pool):
                done = [0]

                def step(ins):
                    done[0] += 1
                    ins.then_inc(consts_step, 1)
                    pool.wait_ge(consts_step, done[0])

                nc.gpsimd.memset(wpad[2][:], 0.0).then_inc(pads_zero, 1)
                nc.gpsimd.memset(wpad[3][:], 0.0).then_inc(pads_zero, 1)
                step(nc.gpsimd.memset(ident[:], 0.0))
                step(nc.gpsimd.affine_select(out=ident[:], in_=ident[:], compare_op=ALU.not_equal, fill=1.0, base=0,
                                             pattern=[[-1, 128]], channel_multiplier=1))
                nc.gpsimd.tensor_copy(identb[:], ident[:]).then_inc(consts, 1)
                step(nc.gpsimd.memset(sel[:], 0.0))
                for part in range(2):
                    step(nc.gpsimd.affine_select(out=sel[:], in_=sel[:], compare_op=ALU.not_equal, fill=1.0,
                                                 base=-GH * part, pattern=[[-1, GH], [0, 128]], channel_multiplier=1))
                step(nc.gpsimd.memset(mask_qk[:], 0.0))
                step(nc.gpsimd.memset(mask_kq[:], 0.0))
                step(nc.gpsimd.affine_select(out=mask_qk[:], in_=mask_qk[:], compare_op=ALU.is_ge, fill=MASKED, base=0,
                                             pattern=[[-1, 128]], channel_multiplier=1))
                step(nc.gpsimd.affine_select(out=mask_kq[:], in_=mask_kq[:], compare_op=ALU.is_ge, fill=MASKED, base=0,
                                             pattern=[[1, 128]], channel_multiplier=-1))
                step(nc.gpsimd.memset(mask1[:], 1.0))
                step(nc.gpsimd.affine_select(out=mask1[:], in_=mask1[:], compare_op=ALU.is_ge, fill=0.0, base=0,
                                             pattern=[[-DH, H], [0, NG]], channel_multiplier=1))
                step(nc.gpsimd.affine_select(out=mask1[:], in_=mask1[:], compare_op=ALU.is_ge, fill=0.0, base=DH - 1,
                                             pattern=[[DH, H], [0, NG]], channel_multiplier=-1))
                m2v = mask2[:, :, :].rearrange("p c (h g) -> p c h g", g=DH)
                step(nc.gpsimd.memset(mask2[:], 1.0))
                step(nc.gpsimd.affine_select(out=m2v, in_=m2v, compare_op=ALU.is_ge, fill=0.0, base=0,
                                             pattern=[[128, 4], [-32, H], [0, DH]], channel_multiplier=1))
                step(nc.gpsimd.affine_select(out=m2v, in_=m2v, compare_op=ALU.is_ge, fill=0.0, base=31,
                                             pattern=[[-128, 4], [32, H], [0, DH]], channel_multiplier=-1))
                nc.gpsimd.memset(m2[:], 0.0)
                nc.gpsimd.memset(vpad[:], 0.0)
                nc.gpsimd.memset(sfrep[:], 0.0)
                nc.gpsimd.memset(wgt[:], 0.0)
                nc.gpsimd.memset(zero[:], 0.0)
                nc.gpsimd.memset(eps[:], EPS)
                nc.gpsimd.memset(lnd[:], -0.5 * math.log(D))
                nc.gpsimd.memset(ones[:], 1.0).then_inc(consts, 1)

            @block.scalar
            def _(act):
                act.wait_ge(weights_in, 16 * 16)
                nc.scalar.activation(silu[:, 0, :], col(0, "cond", 0, B), ACT.Exp, scale=-1.0).then_inc(act_exp_c, 1)
                for n in range(4):
                    act.wait_ge(a0_full, n + 1)
                    nc.scalar.copy(a0[:, 4 * n:4 * n + 4, :], psum[:, n % 2, :]).then_inc(a0_free, 1)

            @block.vector
            def _(dve):
                done = [0]

                def step(ins):
                    done[0] += 1
                    ins.then_inc(setup_step, 1)
                    dve.wait_ge(setup_step, done[0])

                dve.wait_ge(weights_in, 16 * 16)
                dve.wait_ge(act_exp_c, 1)
                step(nc.vector.tensor_scalar(silu[:, 1, :], silu[:, 0, :], 1.0, None, ALU.add))
                step(nc.vector.reciprocal(silu[:, 2, :], silu[:, 1, :]))
                nc.vector.tensor_tensor(silu[:, 0, :], silu[:, 2, :], col(0, "cond", 0, B), ALU.mult).then_inc(silu_ready, 1)
                dve.wait_ge(mods_full, 1)
                bm = col(0, "mods", 0, 14)
                step(nc.vector.tensor_tensor(raw[:, :, :], psum[:, 2, 0:14 * B].rearrange("p (c b) -> p c b", b=B),
                                             bm.unsqueeze(2).broadcast_to([128, 14, B]), ALU.add))

                def mod(i):
                    return mods_all[:, i, :]

                def block_mods(base, sc, sh, gate, bias):
                    nc.vector.tensor_scalar(mod(base), raw[:, sc, :], 1.0, None, ALU.add)
                    nc.vector.tensor_copy(mod(base + 1), raw[:, sh, :])
                    nc.vector.tensor_copy(mod(base + 2), raw[:, gate, :])
                    step(nc.vector.tensor_scalar(mod(base + 3), raw[:, gate, :], bias, None, ALU.mult))

                block_mods(SC0A, 1, 0, 2, col(0, "b_out0"))
                block_mods(SC0B, 4, 3, 5, col(0, "b2_0"))
                block_mods(SC3A, 7, 6, 8, col(0, "bproj"))
                block_mods(SC3B, 10, 9, 11, col(0, "b2_3"))
                for sc, g, be in ((SC3A, "g1", "be1"), (SC3B, "g2", "be2")):
                    step(nc.vector.scalar_tensor_tensor(out=mod(sc + 1), in0=mod(sc), scalar=col(0, be), in1=mod(sc + 1),
                                                        op0=ALU.mult, op1=ALU.add))
                    step(nc.vector.tensor_scalar(mod(sc), mod(sc), col(0, g), None, ALU.mult))
                nc.vector.tensor_scalar(mod(SC2), raw[:, 12, :], col(0, "ln_g"), None, ALU.mult)
                nc.vector.scalar_tensor_tensor(out=mod(SH2), in0=raw[:, 12, :], scalar=col(0, "ln_b"), in1=raw[:, 13, :],
                                               op0=ALU.mult, op1=ALU.add)
                step(nc.vector.memset(mod(G2), 1.0))
                step(nc.vector.tensor_scalar(mod(GB2), mod(G2), col(0, "bp"), None, ALU.mult))
                nc.vector.tensor_scalar(bq1s[:], col(0, "bq1", 0, 2), float(DH) ** -0.5, None, ALU.mult)
                nc.vector.tensor_tensor(bout1[:], col(0, "bout1", 0), col(0, "bout1", 1), ALU.add)
                dve.wait_ge(qw_full, 1)
                nc.vector.tensor_copy(qw_all[:], psum[0:1, 3, 0:B * D]).then_inc(vcopy, 1)
                dve.wait_ge(vcopy, 1)

            @block.tensor
            def _(pe):
                pe.wait_ge(weights_in, 16 * 16)
                pe.wait_ge(silu_ready, 1)
                cond = col(0, "cond", 0, B)
                chunks = [(w0s, W0_AT["mod"][0] + D * c, silu[:, 0, :]) for c in range(6)]
                chunks += [(w3s, W3_AT["ada"][0] + D * c, silu[:, 0, :]) for c in range(6)]
                chunks += [(w2s, W2_AT["gamma"][0], cond), (w2s, W2_AT["beta"][0], cond)]
                for n, (w, at, c) in enumerate(chunks):
                    mm = nc.tensor.matmul(psum[:, 2, B * n:B * n + B], w[:, at:at + D], c, start=True, stop=True)
                mm.then_inc(mods_full, 1)
                wq = w1s[:, W1_AT["self_q"][0]:W1_AT["self_q"][1]]
                for b in range(B):
                    mm = nc.tensor.matmul(psum[0:1, 3, D * b:D * b + D], cond[:, b:b + 1], wq, start=True, stop=True)
                mm.then_inc(qw_full, 1)
                for n in range(4):
                    if n >= 2:
                        pe.wait_ge(a0_free, n - 1)
                    for h in range(4 * n, 4 * n + 4):
                        mm = nc.tensor.matmul(psum[:, n % 2, D * (h % 4):D * (h % 4) + D], wqk0s[:, 0, h, :],
                                              wqk0s[:, 1, h, :], start=True, stop=True)
                    mm.then_inc(a0_full, 1)

        loop_sems = []

        def loop_sem(name):
            s = sem(name)
            loop_sems.append(s)
            return s

        work_full = [loop_sem(f"work_full{i}") for i in range(2)]
        x_loaded = loop_sem("x_loaded")
        adj_loaded = loop_sem("adj_loaded")
        mods_ready = loop_sem("mods_ready")
        stats_ready = loop_sem("stats_ready")
        mv_ready = loop_sem("mv_ready")
        lnv_ready = loop_sem("lnv_ready")
        rstd_ready = loop_sem("rstd_ready")
        xn_ready = loop_sem("xn_ready")
        h_ready = loop_sem("h_ready")
        xb_ready = loop_sem("xb_ready")
        x_ready = loop_sem("x_ready")
        ff_ready = loop_sem("ff_ready")
        hb_ready = loop_sem("hb_ready")
        g_ready = loop_sem("g_ready")
        gb_ready = loop_sem("gb_ready")
        pairsum_ready = loop_sem("pairsum_ready")
        v_by_act = loop_sem("v_by_act")
        v_by_dve = loop_sem("v_by_dve")
        vpad_ready = loop_sem("vpad_ready")
        part1_ready = loop_sem("part1_ready")
        rest_ready = loop_sem("rest_ready")
        part2_ready = loop_sem("part2_ready")
        part3_ready = loop_sem("part3_ready")
        part_in_dram = [[loop_sem(f"part_in_dram_{'qk'[s]}{p}") for p in range(PARTS)] for s in range(2)]
        stack_ready = [loop_sem(f"stack_ready_{'qk'[s]}") for s in range(2)]
        stack_zero = loop_sem("stack_zero")
        s_full = loop_sem("s_full")
        max_done = loop_sem("max_done")
        negm_hi = loop_sem("negm_hi")
        m2_ready = loop_sem("m2_ready")
        mT_ready = loop_sem("mT_ready")
        st_full = loop_sem("st_full")
        pt_ready = loop_sem("pt_ready")
        pt_used = loop_sem("pt_used")
        lnsum_ready = loop_sem("lnsum_ready")
        rden_ready = loop_sem("rden_ready")
        o_done = loop_sem("o_done")
        adjw_ready = loop_sem("adjw_ready")
        cond_step = loop_sem("cond_step")
        nz_ready = loop_sem("nz_ready")
        sf_ready = loop_sem("sf_ready")
        sfrep_ready = loop_sem("sfrep_ready")
        q1_ready = loop_sem("q1_ready")
        kbd_ready = loop_sem("kbd_ready")
        vbd_ready = loop_sem("vbd_ready")
        aff_masked = loop_sem("aff_masked")
        aff_biased = loop_sem("aff_biased")
        amax_ready = loop_sem("amax_ready")
        aff_shifted = loop_sem("aff_shifted")
        aff_exp = loop_sem("aff_exp")
        asum_ready = loop_sem("asum_ready")
        arec_ready = loop_sem("arec_ready")
        wgt_ready = loop_sem("wgt_ready")
        wT_ready = loop_sem("wT_ready")
        y1_done = loop_sem("y1_done")
        y1_sum = loop_sem("y1_sum")
        out_stored = loop_sem("out_stored")
        loop_ids = sorted(s.num for s in loop_sems)
        assert loop_ids == list(range(loop_ids[0], loop_ids[-1] + 1))

        def slot(key):
            return WORK[key] % 2

        def bank(key):
            return psum[:, W_BANK + slot(key), :]

        def wait_full(eng, key):
            eng.wait_ge(work_full[slot(key)], WORK[key] // 2 + 1)

        read_by = {}
        in_order = list(WORK)

        def wait_free(pe, key):
            if WORK[key] >= 2:
                for signal, value in read_by[in_order[WORK[key] - 2]]:
                    pe.wait_ge(signal, value)

        def mod2(i, b):
            return mods[:, i, b:b + 1]

        HEADS_PER_O = {0: 2, 2: 4, 3: 4}
        U_BASE = {0: 0, 2: UNITS, 3: 2 * UNITS}
        O_BASE = {0: 0, 2: 16, 3: 24}
        G_BASE = {0: 0, 2: GROUPS, 3: 2 * GROUPS}
        EXP_SCALE = {0: float(DH0) ** -0.5, 2: 1.0, 3: float(DH) ** -0.5}
        STEPS = UNITS + O_LAG + 1

        def cols_st(layer):
            return NT * T if layer != 3 else T + 128

        def o_at(layer, i):
            v = i - O_LAG
            n = HEADS_PER_O[layer]
            return v // n if 0 <= v < UNITS and v % n == n - 1 else None

        with nc.Fori(0, B // PB) as it:
            with nc.Block() as block:
                @block.sync
                def _(sp):
                    for b in range(PB):
                        sp.dma_start(xT[:, b * T:(b + 1) * T], x_t[it * PB + b]).then_inc(x_loaded, 16)
                    for b in range(PB):
                        for n in range(NT):
                            i = b * NT + n
                            sp.dma_start(adj_s[:, 0, i, :].rearrange("p (m l) -> p m l", l=NL),
                                         adj[it * PB + b, n * 128:(n + 1) * 128, 0:NG, :]).then_inc(adj_loaded, 16)
                    for b in range(PB):
                        for n in range(NT):
                            i = b * NT + n
                            sp.dma_start(adj_s[:, 1, i, :].rearrange("p (m l) -> p m l", l=NL),
                                         adj[it * PB + b, 0:NG, n * 128:(n + 1) * 128, :].rearrange("m p l -> p m l")
                                         ).then_inc(adj_loaded, 16)
                    sp.wait_ge(stack_zero, 1)
                    for a in range(2):
                        for p in range(PARTS):
                            for s in range(2):
                                sp.wait_ge((part1_ready, part2_ready, part3_ready)[p], 2 * a + s + 1)
                                sp.dma_start(scratch[s, p], parts[:, s, p, :]).then_inc(part_in_dram[s][p], 16)
                        for p in range(PARTS):
                            for s in range(2):
                                sp.wait_ge(part_in_dram[s][p], 16 * (a + 1))
                                by_head = scratch[s, p].rearrange("(h d) t -> d h t", d=DH)
                                for o in range(PARTS):
                                    n = PARTS * p + o if s == 0 else PARTS * o + p
                                    sp.dma_start(stacks[DH * n:DH * n + DH, s, :, :], by_head).then_inc(stack_ready[s], 16)
                    sp.wait_ge(x_ready, 14)
                    for b in range(PB):
                        sp.dma_start(out_t[it * PB + b], xT[:, b * T:(b + 1) * T]).then_inc(out_stored, 16)
                    sp.wait_ge(out_stored, 16 * PB)

                @block.gpsimd
                def _(pool):
                    def attention(layer):
                        q0 = 128 if layer == 3 else 0
                        for u in range(U_BASE[layer], U_BASE[layer] + UNITS):
                            pool.wait_ge(pt_ready, u + 1)
                            if u >= 2:
                                pool.wait_ge(pt_used, u - 1)
                            nc.gpsimd.tensor_tensor(pairsum[:, u % 2, q0:T], pt[:, u % PT_RING, q0:T],
                                                    pt[:, u % PT_RING, T:2 * T - q0], ALU.add
                                                    ).then_inc(pairsum_ready, 1)

                    attention(0)
                    pool.wait_ge(pt_used, UNITS)
                    nc.gpsimd.memset(big[64:128, :], 0.0).then_inc(stack_zero, 1)
                    pool.wait_ge(stack_zero, 1)
                    pool.wait_ge(cond_step, 7)
                    for i in l1_steps():
                        if i < 2 * TILES:
                            pool.wait_ge(aff_masked, i + 1)
                            d, t = i % 2, i // 2
                            bias = bias1[:, d, t * NG:(t + 1) * NG].unsqueeze(1).broadcast_to([128, H, NG])
                            nc.gpsimd.tensor_tensor(aff[:, i % 4], aff[:, i % 4], bias, ALU.add).then_inc(aff_biased, 1)
                        if 0 <= i - 1 < 2 * TILES:
                            w = i - 1
                            pool.wait_ge(amax_ready, w + 1)
                            pool.wait_ge(aff_biased, w + 1)
                            nc.gpsimd.tensor_tensor(aff[:, w % 4], aff[:, w % 4],
                                                    amax[:, w % 4, :].unsqueeze(2).broadcast_to([128, H, NG]),
                                                    ALU.subtract).then_inc(aff_shifted, 1)
                        if 0 <= i - 3 < 2 * TILES:
                            w = i - 3
                            pool.wait_ge(arec_ready, w + 1)
                            if w >= 2:
                                wait_full(pool, ("wT", w - 2))
                            nc.gpsimd.tensor_tensor(wgt[:, w % 2, :, 0:NG], aff[:, w % 4],
                                                    arec[:, w % 4, :].unsqueeze(2).broadcast_to([128, H, NG]),
                                                    ALU.mult).then_inc(wgt_ready, 1)
                    attention(2)
                    attention(3)

                @block.scalar
                def _(act):
                    def norm(name):
                        n = LN_ORDER.index(name)
                        act.wait_ge(mv_ready, TILES * (n + 1))
                        nc.scalar.activation(lnv[:], mv[:, :, 1], ACT.Ln, bias=eps[:, 0:1]).then_inc(lnv_ready, 1)
                        act.wait_ge(lnv_ready, n + 1)
                        nc.scalar.activation(rstd[:], lnv[:], ACT.Exp, scale=-0.5).then_inc(rstd_ready, 1)

                    def attention(layer):
                        width = cols_st(layer)
                        for i in range(STEPS):
                            if i >= GH + 1 and (i - GH - 1) % GH == 0 and (i - GH - 1) // GH < GROUPS:
                                g = (i - GH - 1) // GH
                                key = ("mT", layer, g)
                                wait_full(act, key)
                                nc.scalar.copy(mT[:, g % 2, :], bank(key)[:, 0:T // 2].bitcast(BF16)
                                               ).then_inc(mT_ready, 1)
                                read_by[key] = [(mT_ready, G_BASE[layer] + g + 1)]
                            if 0 <= i - ST_LAG < UNITS:
                                u = U_BASE[layer] + i - ST_LAG
                                act.wait_ge(st_full, u + 1)
                                if u >= PT_RING:
                                    act.wait_ge(pt_used, u - PT_RING + 1)
                                nc.scalar.activation(pt[:, u % PT_RING, 0:width], psum[:, ST_BANK + u % 2, 0:width],
                                                     ACT.Exp, scale=EXP_SCALE[layer]).then_inc(pt_ready, 1)
                            o = o_at(layer, i)
                            if o is not None:
                                o += O_BASE[layer]
                                act.wait_ge(pt_used, U_BASE[layer] + i - O_LAG + 1)
                                if o >= 2:
                                    act.wait_ge(o_done, o - 1)
                                nc.scalar.activation(rden[:, o % 2, :], psum[:, O_BANK + o % 2, T:2 * T],
                                                     ACT.Ln).then_inc(lnsum_ready, 1)
                                act.wait_ge(lnsum_ready, o + 1)
                                nc.scalar.activation(rden[:, o % 2, :], rden[:, o % 2, :], ACT.Exp, scale=-1.0,
                                                     bias=(lnd if layer == 2 else zero)[:, 0:1]).then_inc(rden_ready, 1)

                    def mlp(layer):
                        nc.scalar.preload_act_table_set("gelu_and_others")
                        for c in range(FC):
                            key = ("ff", layer, c)
                            wait_full(act, key)
                            nc.scalar.activation(ff[:, c, :], bank(key), ACT.Gelu,
                                                 bias=col(0, "b1_0" if layer == 0 else "b1_3", c)
                                                 ).then_inc(ff_ready, 1)
                            read_by[key] = [(ff_ready, c + 1 + (FC if layer else 0))]
                        nc.scalar.preload_act_table_set(EXP_LN_SET)

                    nc.scalar.preload_act_table_set(EXP_LN_SET)
                    norm("0a")
                    act.wait_ge(h_ready, PB)
                    nc.scalar.copy(hTb[:], hT[:]).then_inc(hb_ready, 1)
                    for h in range(H):
                        act.wait_ge(g_ready, h + 1)
                        nc.scalar.copy(gTb[:, h, :], gT[:, h, :]).then_inc(gb_ready, 1)
                    for t in range(TILES):
                        wait_full(act, ("V", t, 0))
                        nc.scalar.copy(v0[:, t, 0:512], bank(("V", t, 0))).then_inc(v_by_act, 1)
                        read_by["V", t, 0] = [(v_by_act, t + 1)]
                    attention(0)
                    norm("0b")
                    mlp(0)
                    wait_full(act, "sf")
                    nc.scalar.activation(sfT[:], bank("sf"), ACT.Identity, bias=col(0, "b_self")).then_inc(sf_ready, 1)
                    read_by["sf"] = [(sf_ready, 1)]
                    for d in range(2):
                        wait_full(act, ("q1", d))
                        nc.scalar.activation(q1T[:, d, :], bank(("q1", d)), ACT.Identity, bias=bq1s[:, d:d + 1],
                                             scale=float(DH) ** -0.5).then_inc(q1_ready, 1)
                        read_by["q1", d] = [(q1_ready, d + 1)]
                    for i in l1_steps():
                        if 0 <= i - 2 < 2 * TILES:
                            w = i - 2
                            act.wait_ge(aff_shifted, w + 1)
                            nc.scalar.activation(aff[:, w % 4], aff[:, w % 4], ACT.Exp).then_inc(aff_exp, 1)
                        if 0 <= i - 4 < 2 * TILES:
                            w = i - 4
                            wait_full(act, ("wT", w))
                            if w >= 2:
                                act.wait_ge(y1_done, w - 1)
                            nc.scalar.copy(wT[:, w % 2, :], bank(("wT", w))).then_inc(wT_ready, 1)
                            read_by["wT", w] = [(wT_ready, w + 1)]
                    for a, layer in enumerate((2, 3)):
                        norm(f"{layer}a")
                        for s, name in enumerate("qk"):
                            key = (name, layer)
                            wait_full(act, key)
                            nc.scalar.activation(parts[:, s, 0, :], bank(key), ACT.Identity,
                                                 bias=col(0, f"b{name}2") if layer == 2 else zero[:, 0:1]
                                                 ).then_inc(part1_ready, 1)
                        for s in range(2):
                            act.wait_ge(rest_ready, 2 * a + s + 1)
                            nc.scalar.copy(parts[:, s, 1, :], rest[:, s, :]).then_inc(part2_ready, 1)
                        attention(layer)
                        norm(f"{layer}b")
                    mlp(3)

                @block.vector
                def _(dve):
                    x_updates = [0]
                    xb_steps = [0]
                    h_steps = [0]

                    def norm(name, sc, into_x=False):
                        n = LN_ORDER.index(name)
                        tok, fm = ("tok", name), ("fm", name)
                        wait_full(dve, tok)
                        for t in range(TILES):
                            nc.vector.bn_stats(stats[:, t, :], bank(tok)[:, t * 128:(t + 1) * 128]).then_inc(stats_ready, 1)
                        for t in range(TILES):
                            dve.wait_ge(stats_ready, TILES * n + t + 1)
                            nc.vector.bn_aggr(mv[:, t, :], stats[:, t, :]).then_inc(mv_ready, 1)
                        dve.wait_ge(rstd_ready, n + 1)
                        for t in range(TILES):
                            ins = nc.vector.tensor_scalar(xn[:, t, :], bank(tok)[:, t * 128:(t + 1) * 128], mv[:, t, 0:1],
                                                          rstd[:, t:t + 1], ALU.subtract, ALU.mult)
                            ins.then_inc(xn_ready, 1)
                        read_by[tok] = [(xn_ready, TILES * (n + 1))]
                        if into_x:
                            residual(sc + 1)
                        wait_full(dve, fm)
                        for b in range(PB):
                            cols = slice(b * T, (b + 1) * T)
                            if into_x:
                                ins = nc.vector.scalar_tensor_tensor(out=xT[:, cols], in0=bank(fm)[:, cols],
                                                                     scalar=mod2(sc, b), in1=xb[:, cols],
                                                                     op0=ALU.mult, op1=ALU.add)
                                x_updates[0] += 1
                                ins.then_inc(x_ready, 1)
                            else:
                                ins = nc.vector.tensor_scalar(hT[:, cols], bank(fm)[:, cols], mod2(sc, b), mod2(sc + 1, b),
                                                              ALU.mult, ALU.add)
                                h_steps[0] += 1
                                ins.then_inc(h_ready, 1)
                        read_by[fm] = [(x_ready, x_updates[0]) if into_x else (h_ready, h_steps[0])]

                    def residual(gb):
                        dve.wait_ge(x_ready, x_updates[0])
                        for b in range(PB):
                            cols = slice(b * T, (b + 1) * T)
                            xb_steps[0] += 1
                            nc.vector.tensor_scalar(xb[:, cols], xT[:, cols], mod2(gb, b), None, ALU.add
                                                    ).then_inc(xb_ready, 1)
                        dve.wait_ge(xb_ready, xb_steps[0])

                    def gated(key, gate):
                        wait_full(dve, key)
                        for b in range(PB):
                            cols = slice(b * T, (b + 1) * T)
                            x_updates[0] += 1
                            nc.vector.scalar_tensor_tensor(out=xT[:, cols], in0=bank(key)[:, cols], scalar=mod2(gate, b),
                                                           in1=xb[:, cols], op0=ALU.mult, op1=ALU.add
                                                           ).then_inc(x_ready, 1)
                        read_by[key] = [(x_ready, x_updates[0])]

                    def attention(layer):
                        for i in range(STEPS):
                            if i < UNITS:
                                u = U_BASE[layer] + i
                                g, j = i // GH, i % GH
                                bk = psum[:, S_BANK + u % 2, :]
                                dve.wait_ge(s_full, u + 1)
                                if layer == 3:
                                    nc.vector.tensor_reduce(negm[:, g % 2, 0, j:j + 1], bk[:, 0:128], AX_X, ALU.max,
                                                            negate=True)
                                    ins = nc.vector.tensor_reduce(negm[:, g % 2, 1, j:j + 1], bk[:, 128:384], AX_X,
                                                                  ALU.max, negate=True)
                                else:
                                    ins = nc.vector.tensor_reduce(negm[:, g % 2, :, j],
                                                                  bk.rearrange("p (q k) -> p q k", q=NT), AX_X,
                                                                  ALU.max, negate=True)
                                ins.then_inc(max_done, 1)
                                if j == GH - 1:
                                    dve.wait_ge(max_done, u + 1)
                                    if g >= 2:
                                        wait_full(dve, ("mT", layer, g - 2))
                                    hi, lo = m2[:, g % 2, :, 0:GH], m2[:, g % 2, :, GH:2 * GH]
                                    nc.vector.tensor_copy(hi, negm[:, g % 2]).then_inc(negm_hi, 1)
                                    dve.wait_ge(negm_hi, G_BASE[layer] + g + 1)
                                    nc.vector.tensor_tensor(lo, negm[:, g % 2], hi, ALU.subtract).then_inc(m2_ready, 1)
                            o = o_at(layer, i)
                            if o is not None:
                                n = H // HEADS_PER_O[layer]
                                b, c = o // n, o % n
                                o += O_BASE[layer]
                                dve.wait_ge(rden_ready, o + 1)
                                nc.vector.tensor_tensor(oT[:, c, b * T:(b + 1) * T], psum[:, O_BANK + o % 2, 0:T],
                                                        rden[:, o % 2, :], ALU.mult).then_inc(o_done, 1)

                    nc.vector.tensor_copy(mods[:], mods_all[:, :, bass.ds(it * PB, PB)]).then_inc(mods_ready, 1)
                    nc.vector.tensor_copy(qw[:], qw_all[:, bass.ds(it * PB, PB), :]).then_inc(mods_ready, 1)
                    dve.wait_ge(mods_ready, 2)
                    dve.wait_ge(x_loaded, 16 * PB)
                    norm("0a", SC0A)
                    for h in range(H):
                        wait_full(dve, ("G", h))
                        nc.vector.tensor_copy(gT[:, h, :], bank(("G", h))).then_inc(g_ready, 1)
                        read_by["G", h] = [(g_ready, h + 1)]
                    for t in range(TILES):
                        wait_full(dve, ("V", t, 1))
                        nc.vector.tensor_copy(v0[:, t, 512:1024], bank(("V", t, 1))).then_inc(v_by_dve, 1)
                        read_by["V", t, 1] = [(v_by_dve, t + 1)]
                    residual(GB0A)
                    attention(0)
                    gated(("proj", 0), G0A)
                    norm("0b", SC0B)
                    residual(GB0B)
                    gated(("y", 0), G0B)

                    dve.wait_ge(adj_loaded, 16 * 2 * TILES)
                    wb = wbias[:, 0:NL].unsqueeze(1).broadcast_to([128, TILES * NG, NL])
                    for d in range(2):
                        nc.vector.tensor_tensor(adj_w[:, d], adj_s[:, d].rearrange("p i (m l) -> p (i m) l", l=NL), wb,
                                                ALU.mult).then_inc(adjw_ready, 1)
                    for d in range(2):
                        nc.vector.tensor_reduce(cond1[:, d], adj_s[:, d].rearrange("p i (m l) -> p (i m) l", l=NL), AX_X,
                                                ALU.add).then_inc(cond_step, 1)
                    for d in range(2):
                        dve.wait_ge(adjw_ready, d + 1)
                        nc.vector.tensor_reduce(vb1[:, d], adj_w[:, d], AX_X, ALU.add).then_inc(cond_step, 1)
                    dve.wait_ge(cond_step, 2)
                    nc.vector.tensor_scalar(keep1[:], cond1[:], 0.0, None, ALU.is_gt).then_inc(cond_step, 1)
                    dve.wait_ge(cond_step, 5)
                    nc.vector.tensor_scalar(cond1[:], keep1[:], 1.0, -NEG, ALU.subtract, ALU.mult).then_inc(cond_step, 1)
                    dve.wait_ge(cond_step, 6)
                    nc.vector.scalar_tensor_tensor(out=bias1[:], in0=vb1[:], scalar=wbias[:, NL:NL + 1], in1=cond1[:],
                                                   op0=ALU.add, op1=ALU.add).then_inc(cond_step, 1)
                    wait_full(dve, "nz")
                    nc.vector.tensor_scalar(nz[:], bank("nz")[0:1, :], 0.0, None, ALU.not_equal).then_inc(nz_ready, 1)
                    read_by["nz"] = [(nz_ready, 1)]
                    dve.wait_ge(sf_ready, 1)
                    for b in range(PB):
                        nc.vector.tensor_copy(sfrep[:, b, :, 0:NG],
                                              sfT[:, b * T:b * T + NG].unsqueeze(1).broadcast_to([128, 4, NG])
                                              ).then_inc(sfrep_ready, 1)
                    nc.vector.tensor_scalar(sfb[:], sfT[:], bout1[:, 0:1], None, ALU.add).then_inc(sfrep_ready, 1)
                    wait_full(dve, "k1")
                    for d in range(2):
                        for b in range(PB):
                            src = bank("k1")[:, (d * PB + b) * NG:(d * PB + b + 1) * NG].unsqueeze(1)
                            nc.vector.scalar_tensor_tensor(out=kbd[:, d, b, :].rearrange("p (h m) -> p h m", h=H),
                                                           in0=src.broadcast_to([128, H, NG]), scalar=col(0, "bk1", d),
                                                           in1=mask1[:], op0=ALU.add, op1=ALU.mult).then_inc(kbd_ready, 1)
                    read_by["k1"] = [(kbd_ready, 4)]
                    wait_full(dve, "v1")
                    for d in range(2):
                        for b in range(PB):
                            src = bank("v1")[:, (d * PB + b) * D:(d * PB + b + 1) * D].unsqueeze(1)
                            nc.vector.tensor_tensor(vbd[:, d, b, :].rearrange("p (c n) -> p c n", c=4),
                                                    src.broadcast_to([128, 4, D]), mask2[:], ALU.mult
                                                    ).then_inc(vbd_ready, 1)
                    read_by["v1"] = [(vbd_ready, 4)]
                    for i in l1_steps():
                        if i < 2 * TILES:
                            d, t = i % 2, i // 2
                            wait_full(dve, ("s1", i))
                            if i >= 4:
                                dve.wait_ge(wgt_ready, i - 3)
                            keep = keep1[:, d, t * NG:(t + 1) * NG].unsqueeze(1).broadcast_to([128, H, NG])
                            nc.vector.tensor_tensor(aff[:, i % 4], bank(("s1", i))[:, 0:H * NG].rearrange(
                                "p (h m) -> p h m", h=H), keep, ALU.mult).then_inc(aff_masked, 1)
                            read_by["s1", i] = [(aff_masked, i + 1)]
                        if 0 <= i - 1 < 2 * TILES:
                            w = i - 1
                            dve.wait_ge(aff_biased, w + 1)
                            nc.vector.tensor_reduce(amax[:, w % 4, :], aff[:, w % 4], AX_X, ALU.max).then_inc(amax_ready, 1)
                        if 0 <= i - 2 < 2 * TILES:
                            w = i - 2
                            dve.wait_ge(aff_exp, w + 1)
                            nc.vector.tensor_reduce(asum[:, w % 4, :], aff[:, w % 4], AX_X, ALU.add).then_inc(asum_ready, 1)
                            dve.wait_ge(asum_ready, w + 1)
                            nc.vector.reciprocal(arec[:, w % 4, :], asum[:, w % 4, :]).then_inc(arec_ready, 1)
                    dve.wait_ge(y1_done, 2 * TILES)
                    nc.vector.tensor_tensor(sfb[:], psum[:, O_BANK, :], sfb[:], ALU.add).then_inc(y1_sum, 1)
                    dve.wait_ge(y1_sum, 1)
                    nc.vector.scalar_tensor_tensor(out=xT[:], in0=sfb[:], scalar=0.0, in1=xT[:], op0=ALU.max,
                                                   op1=ALU.add).then_inc(x_ready, 2)
                    x_updates[0] += 2

                    for a, layer in enumerate((2, 3)):
                        dve.wait_ge(x_ready, x_updates[0])
                        norm(f"{layer}a", SC2 if layer == 2 else SC3A)
                        for s, name in enumerate("qk"):
                            key = (name, layer)
                            dve.wait_ge(part1_ready, 2 * a + s + 1)
                            nc.vector.scalar_tensor_tensor(out=rest[:, s, :], in0=bank(key),
                                                           scalar=col(0, f"b{name}2") if layer == 2 else zero[:, 0:1],
                                                           in1=parts[:, s, 0, :], op0=ALU.add, op1=ALU.subtract
                                                           ).then_inc(rest_ready, 1)
                            read_by[key] = [(rest_ready, 2 * a + s + 1)]
                        for s in range(2):
                            dve.wait_ge(part2_ready, 2 * a + s + 1)
                            nc.vector.tensor_tensor(parts[:, s, 2, :], rest[:, s, :], parts[:, s, 1, :], ALU.subtract
                                                    ).then_inc(part3_ready, 1)
                        key = ("v", layer)
                        wait_full(dve, key)
                        src = bank(key).rearrange("p (t h d) -> p t h d", t=TILES, h=H)
                        for t in range(TILES):
                            if layer == 2:
                                ins = nc.vector.tensor_tensor(vpad[:, t, :, 0:DH], src[:, t],
                                                              bv2[:, :].rearrange("p (h d) -> p h d", h=H), ALU.add)
                            else:
                                ins = nc.vector.tensor_copy(vpad[:, t, :, 0:DH], src[:, t])
                            ins.then_inc(vpad_ready, 1)
                        read_by[key] = [(vpad_ready, TILES * (a + 1))]
                        residual(GB2 if layer == 2 else GB3A)
                        attention(layer)
                        gated(("proj", layer), G2 if layer == 2 else G3A)
                        norm(f"{layer}b", SC2 if layer == 2 else SC3B, into_x=layer == 2)
                    residual(GB3B)
                    gated(("y", 3), G3B)

                @block.tensor
                def _(pe):
                    def done(ins, key):
                        ins.then_inc(work_full[slot(key)], 1)

                    def norm(name):
                        n = LN_ORDER.index(name)
                        if n:
                            pe.wait_ge(x_ready, {"0b": 2, "2a": 6, "2b": 8, "3a": 10, "3b": 12}[name])
                        else:
                            pe.wait_ge(x_loaded, 16 * PB)
                        key = ("tok", name)
                        wait_free(pe, key)
                        for t in range(TILES):
                            ins = nc.tensor.transpose(bank(key)[:, t * 128:(t + 1) * 128], xT[:, t * 128:(t + 1) * 128],
                                                      ident[:])
                        done(ins, key)
                        key = ("fm", name)
                        wait_free(pe, key)
                        pe.wait_ge(xn_ready, TILES * (n + 1))
                        for t in range(TILES):
                            ins = nc.tensor.transpose(bank(key)[:, t * 128:(t + 1) * 128], xn[:, t, :], ident[:])
                        done(ins, key)

                    def attention(layer):
                        hpo = HEADS_PER_O[layer]

                        def of(i):
                            return i // H, i % H

                        def scores(i):
                            u = U_BASE[layer] + i
                            b, h = of(i)
                            bk = psum[:, S_BANK + u % 2, :]
                            if u >= 2:
                                pe.wait_ge(max_done, u - 1)
                            keys = hTb[:, b * T:(b + 1) * T] if layer == 0 else stacks[:, 1, h, b * T:(b + 1) * T]
                            qs = gTb[:, h, :] if layer == 0 else stacks[:, 0, h, :]
                            if layer == 0:
                                pe.wait_ge(hb_ready, 1)
                                pe.wait_ge(gb_ready, h + 1)
                            for q in range(NT):
                                lhs = qs[:, b * T + q * 128:b * T + (q + 1) * 128]
                                if layer != 3:
                                    ins = nc.tensor.matmul(bk[:, q * T:(q + 1) * T], lhs, keys, start=True, stop=True)
                                else:
                                    at = q * 128
                                    nc.tensor.matmul(bk[:, at:at + (q + 1) * 128], lhs, keys[:, 0:(q + 1) * 128],
                                                     start=True, stop=False)
                                    ins = nc.tensor.matmul(bk[:, at + q * 128:at + (q + 1) * 128], identb[:], mask_qk[:],
                                                           start=False, stop=True)
                            ins.then_inc(s_full, 1)

                        def shift_rows(g):
                            key = ("mT", layer, g)
                            wait_free(pe, key)
                            pe.wait_ge(m2_ready, G_BASE[layer] + g + 1)
                            dst = bank(key)[:, 0:T // 2].bitcast(BF16)
                            for q in range(NT):
                                ins = nc.tensor.transpose(dst[:, q * 128:(q + 1) * 128], m2[:, g % 2, q, :], identb[:])
                            done(ins, key)

                        def scores_t(i):
                            u = U_BASE[layer] + i
                            b, h = of(i)
                            g, j = i // GH, i % GH
                            bk = psum[:, ST_BANK + u % 2, :]
                            if u >= 2:
                                pe.wait_ge(pt_ready, u - 1)
                            if layer == 0:
                                pe.wait_ge(g_ready, h + 1)
                            if j == 0:
                                pe.wait_ge(mT_ready, G_BASE[layer] + g + 1)
                            shift = mT[:, g % 2, :]
                            for k in range(NT):
                                if layer == 0:
                                    lhs, rhs = hT[:, b * T + k * 128:b * T + (k + 1) * 128], gT[:, h, b * T:(b + 1) * T]
                                else:
                                    lhs = stacks[:, 1, h, b * T + k * 128:b * T + (k + 1) * 128]
                                    rhs = stacks[:, 0, h, b * T:(b + 1) * T]
                                q0 = k * 128 if layer == 3 else 0
                                at = k * T
                                dst = bk[:, at:at + T - q0]
                                nc.tensor.matmul(dst, lhs, rhs[:, q0:T], start=True, stop=False)
                                if layer == 3:
                                    nc.tensor.matmul(bk[:, at:at + 128], identb[:], mask_kq[:], start=False, stop=False)
                                ins = nc.tensor.matmul(dst, sel[:, j, :], shift[:, q0:T], start=False, stop=True)
                            ins.then_inc(st_full, 1)

                        def values(i):
                            u = U_BASE[layer] + i
                            b, h = of(i)
                            o = O_BASE[layer] + i // hpo
                            bk = psum[:, O_BANK + o % 2, :]
                            m = 128 // hpo
                            at = m * (i % hpo)
                            if i == 0 and layer == 0:
                                pe.wait_ge(v_by_act, TILES)
                                pe.wait_ge(v_by_dve, TILES)
                            if i == 0 and layer != 0:
                                pe.wait_ge(vpad_ready, TILES * (1 if layer == 2 else 2))
                            if i % hpo == 0 and o >= 2:
                                pe.wait_ge(o_done, o - 1)
                            pe.wait_ge(pt_ready, u + 1)
                            for k in range(NT):
                                if layer == 0:
                                    lhs = v0[:, b * NT + k, h * DH0:(h + 1) * DH0]
                                else:
                                    lhs = vpad[:, b * NT + k, h, :]
                                q0 = k * 128 if layer == 3 else 0
                                nc.tensor.matmul(bk[at:at + m, q0:T], lhs, pt[:, u % PT_RING, k * T:(k + 1) * T - q0],
                                                 start=(k == 0), stop=(k == NT - 1))
                            q0 = 128 if layer == 3 else 0
                            if q0:
                                nc.tensor.matmul(bk[at:at + m, T:T + q0], ones[:, 0:m], pt[:, u % PT_RING, 0:q0],
                                                 start=True, stop=True)
                            pe.wait_ge(pairsum_ready, u + 1)
                            ins = nc.tensor.matmul(bk[at:at + m, T + q0:2 * T], ones[:, 0:m], pairsum[:, u % 2, q0:T],
                                                   start=True, stop=True)
                            ins.then_inc(pt_used, 1)

                        if layer != 0:
                            a = (2, 3).index(layer)
                            for s in range(2):
                                pe.wait_ge(stack_ready[s], 16 * SLOTS * (a + 1))
                        for i in range(STEPS):
                            if i < UNITS:
                                scores(i)
                            if i >= GH + 1 and (i - GH - 1) % GH == 0 and (i - GH - 1) // GH < GROUPS:
                                shift_rows((i - GH - 1) // GH)
                            if 0 <= i - ST_LAG < UNITS:
                                scores_t(i - ST_LAG)
                            if 0 <= i - PV_LAG < UNITS:
                                values(i - PV_LAG)
                        chunks = H // hpo
                        key = ("proj", layer)
                        wait_free(pe, key)
                        pe.wait_ge(o_done, O_BASE[layer] + PB * chunks)
                        w = (w0s[:, W0_AT["out"][0]:W0_AT["out"][1]].rearrange("p (c n) -> p c n", c=8) if layer == 0
                             else wpad[layer])
                        for c in range(chunks):
                            ins = nc.tensor.matmul(bank(key), w[:, c, :], oT[:, c, :], start=(c == 0), stop=(c == chunks - 1))
                        done(ins, key)

                    def mlp(layer):
                        ws, at = (w0s, W0_AT) if layer == 0 else (w3s, W3_AT)
                        pe.wait_ge(h_ready, 4 if layer == 0 else 10)
                        for c in range(FC):
                            key = ("ff", layer, c)
                            wait_free(pe, key)
                            done(nc.tensor.matmul(bank(key), ws[:, at["w1"][0] + c * 128:at["w1"][0] + (c + 1) * 128], hT[:],
                                                  start=True, stop=True), key)
                        key = ("y", layer)
                        wait_free(pe, key)
                        for c in range(FC):
                            pe.wait_ge(ff_ready, c + 1 + (FC if layer else 0))
                            ins = nc.tensor.matmul(bank(key), ws[:, at["w2"][0] + c * 128:at["w2"][0] + (c + 1) * 128],
                                                   ff[:, c, :], start=(c == 0), stop=(c == FC - 1))
                        done(ins, key)

                    norm("0a")
                    pe.wait_ge(h_ready, 2)
                    for h in range(H):
                        key = ("G", h)
                        wait_free(pe, key)
                        done(nc.tensor.matmul(bank(key), a0[:, h, :], hT[:], start=True, stop=True), key)
                    for t in range(TILES):
                        for n in range(2):
                            key = ("V", t, n)
                            wait_free(pe, key)
                            at = W0_AT["v"][0] + 512 * n
                            done(nc.tensor.matmul(bank(key), hT[:, t * 128:(t + 1) * 128], w0s[:, at:at + 512],
                                                  start=True, stop=True), key)
                    attention(0)
                    norm("0b")
                    mlp(0)

                    def w1(name, d=0):
                        at = W1_AT[name][0] + d * D
                        return w1s[:, at:at + D]

                    pe.wait_ge(x_ready, 4)
                    wait_free(pe, "nz")
                    done(nc.tensor.matmul(bank("nz")[0:1, :], ones[:, 0:1], xT[:], start=True, stop=True), "nz")
                    wait_free(pe, "sf")
                    nc.tensor.matmul(bank("sf"), w1("self_v"), xT[:], start=True, stop=False)
                    pe.wait_ge(nz_ready, 1)
                    for b in range(PB):
                        ins = nc.tensor.matmul(bank("sf")[:, b * T:(b + 1) * T], qw[:, b, :], nz[:, b * T:(b + 1) * T],
                                               start=False, stop=(b == PB - 1))
                    done(ins, "sf")
                    pe.wait_ge(sf_ready, 1)
                    for d in range(2):
                        wait_free(pe, ("q1", d))
                        done(nc.tensor.matmul(bank(("q1", d)), w1("q", d), sfT[:], start=True, stop=True), ("q1", d))
                    wait_free(pe, "k1")
                    nodes = sfT[:, :].rearrange("p (b t) -> p b t", b=PB)[:, :, 0:NG]
                    for d in range(2):
                        ins = nc.tensor.matmul(bank("k1")[:, d * PB * NG:(d + 1) * PB * NG], w1("k", d), nodes,
                                               start=True, stop=True)
                    done(ins, "k1")
                    wait_free(pe, "v1")
                    pe.wait_ge(sfrep_ready, PB)
                    for d in range(2):
                        for b in range(PB):
                            at = (d * PB + b) * D
                            ins = nc.tensor.matmul(bank("v1")[:, at:at + D], sfrep[:, b].rearrange("p h m -> p (h m)"),
                                                   w1("out", d), start=True, stop=True)
                    done(ins, "v1")
                    for i in l1_steps():
                        if i < 2 * TILES:
                            d, t = i % 2, i // 2
                            key = ("s1", i)
                            wait_free(pe, key)
                            if i == 0:
                                pe.wait_ge(q1_ready, 2)
                                pe.wait_ge(kbd_ready, 4)
                            done(nc.tensor.matmul(bank(key)[:, 0:H * NG], q1T[:, d, t * 128:(t + 1) * 128],
                                                  kbd[:, d, t // NT, :], start=True, stop=True), key)
                        if 0 <= i - 4 < 2 * TILES:
                            w = i - 4
                            key = ("wT", w)
                            wait_free(pe, key)
                            pe.wait_ge(wgt_ready, w + 1)
                            for c in range(4):
                                ins = nc.tensor.transpose(bank(key)[:, c * 128:(c + 1) * 128],
                                                          wgt[:, w % 2, 4 * c:4 * c + 4, :].rearrange("p h m -> p (h m)"),
                                                          ident[:])
                            done(ins, key)
                        if 0 <= i - 5 < 2 * TILES:
                            w = i - 5
                            d, t = w % 2, w // 2
                            pe.wait_ge(wT_ready, w + 1)
                            if w == 0:
                                pe.wait_ge(vbd_ready, 4)
                            for c in range(4):
                                ins = nc.tensor.matmul(psum[:, O_BANK, t * 128:(t + 1) * 128],
                                                       vbd[:, d, t // NT, c * D:(c + 1) * D],
                                                       wT[:, w % 2, c * 128:(c + 1) * 128],
                                                       start=(d == 0 and c == 0), stop=(d == 1 and c == 3))
                            ins.then_inc(y1_done, 1)

                    for layer in (2, 3):
                        norm(f"{layer}a")
                        ws, at = (w2s, W2_AT) if layer == 2 else (w3s, W3_AT)
                        pe.wait_ge(h_ready, 6 if layer == 2 else 8)
                        for name in "qk":
                            key = (name, layer)
                            wait_free(pe, key)
                            done(nc.tensor.matmul(bank(key), ws[:, at[name][0]:at[name][1]], hT[:], start=True, stop=True),
                                 key)
                        key = ("v", layer)
                        wait_free(pe, key)
                        for t in range(TILES):
                            ins = nc.tensor.matmul(bank(key)[:, t * D:(t + 1) * D], hT[:, t * 128:(t + 1) * 128],
                                                   ws[:, at["v"][0]:at["v"][1]], start=True, stop=True)
                        done(ins, key)
                        attention(layer)
                        norm(f"{layer}b")
                    mlp(3)

            nc.all_engine_barrier(sems_to_clear=range(loop_ids[0], loop_ids[-1] + 1))


def kernel(**inputs):
    import numpy as np
    import concourse.bacc as bacc
    from concourse.bass_utils import run_bass_kernel_spmd

    a = {k: np.asarray(v) for k, v in inputs.items()}

    def pack(*blocks):
        return np.ascontiguousarray(np.concatenate(blocks, axis=1))

    def heads_out(w):
        c = w.shape[0] // 128
        return w.reshape(c, 128, w.shape[1]).transpose(1, 0, 2).reshape(128, c * w.shape[1])

    def vcols(*vectors):
        return [v.reshape(-1, 128).T for v in vectors]

    qkv0 = a["L0_cond_W_qkv"]
    hd = H * DH0
    wqk0 = np.stack([qkv0[:, 0:hd].T.reshape(H, DH0, D), qkv0[:, hd:2 * hd].T.reshape(H, DH0, D)])
    w2qkv = a["L2_cond_Wqkv"].reshape(D, 3, D)
    b2qkv = a["L2_cond_bqkv"].reshape(D, 3)
    self_t = a["L1_cond_W_self"].T
    mod2 = pack(*vcols(a["L0_cond_b_mod"], a["L3_cond_bada"], a["L2_cond_bg"], a["L2_cond_bb"]))
    arrays = {
        "x_t": a["x"].transpose(0, 2, 1),
        "adj": a["mask_BxSxSx11_ik0"],
        "w0": pack(a["L0_cond_W_mod"], qkv0[:, 2 * hd:], heads_out(a["L0_cond_W_out"]), a["L0_cond_W1"],
                   heads_out(a["L0_cond_W2"])),
        "wqk0": wqk0.transpose(2, 0, 1, 3),
        "w1": pack(self_t[0:D], self_t[D:], *[a["L1_cond_Wq"][d].T for d in range(2)],
                   *[a["L1_cond_Wk"][d].T for d in range(2)],
                   *[a["L1_cond_Wout"][d].reshape(D, D).T for d in range(2)]),
        "w2": pack(a["L2_cond_Wg"].T, a["L2_cond_Wb"].T, *[w2qkv[:, c].T for c in range(3)]),
        "w3": pack(a["L3_cond_Wqkv"], a["L3_cond_W1"], heads_out(a["L3_cond_W2"]), a["L3_cond_Wada"]),
        "wp2": a["L2_cond_Wp"].T,
        "wproj3": a["L3_cond_Wproj"],
        "vecs": pack(mod2, *vcols(
            a["L0_cond_b_out"], a["L0_cond_b2"], a["L0_cond_b1"], a["L1_cond_b_self"], a["L1_cond_bq"], a["L1_cond_bk"],
            a["L1_cond_bout"], a["L2_cond_ln_g"], a["L2_cond_ln_b"], b2qkv[:, 0], b2qkv[:, 1], a["L2_cond_bp"],
            a["L3_cond_bproj"], a["L3_cond_b2"], a["L3_cond_b1"], a["L3_cond_g1"], a["L3_cond_be1"], a["L3_cond_g2"],
            a["L3_cond_be2"], a["cond_1024"])),
        "rows": np.concatenate([b2qkv[:, 2], a["L1_cond_w_bias"], a["L1_cond_b_bias"].reshape(1)]).reshape(1, -1),
    }
    nc = bacc.Bacc("TRN2", target_bir_lowering=False, num_devices=1)
    args = {}
    for name, v in arrays.items():
        arrays[name] = v = np.ascontiguousarray(v)
        args[name] = nc.dram_tensor(name, v.shape, mybir.dt.from_np(v.dtype), kind="ExternalInput").ap()
    out_t = nc.dram_tensor("out_t", (B, D, T), F32, kind="ExternalOutput").ap()
    cond_seq_kernel(nc, out_t=out_t, **args)
    r = run_bass_kernel_spmd(nc, [arrays], core_ids=[0])
    return np.ascontiguousarray(r.results[0]["out_t"].transpose(0, 2, 1))
```

```python
import math
from contextlib import ExitStack

import concourse.bass as bass
from concourse import mybir

ALU = mybir.AluOpType
ACT = mybir.ActivationFunctionType
AX_X = mybir.AxisListType.X
F32 = mybir.dt.float32
BF16 = mybir.dt.bfloat16
I32 = mybir.dt.int32

B, T, D = 4, 256, 128
ROOMS = 2
H_ROOMS = 3
NT = T // 128
H = 16
DH0 = 64
DH = D // H
FF = 512
FC = FF // 128
NG, NL = 20, 11
NEG = -9000000000000000.0
MASKED = -1.0e30
EPS = 1e-5

W0_COLS = dict(mod=6 * D, v=H * DH0, out=8 * D, w1=FF, w2=FF)
W1_COLS = dict(self_v=D, self_q=D, q=2 * D, k=2 * D, out=2 * D)
W2_COLS = dict(gamma=D, beta=D, q=D, k=D, v=D)
W3_COLS = dict(q=D, k=D, v=D, w1=FF, w2=FF, ada=6 * D)
VEC_COLS = dict(mods=14, b_out0=1, b2_0=1, b1_0=4, b_self=1, bq1=2, bk1=2, bout1=2,
                ln_g=1, ln_b=1, bq2=1, bk2=1, bp=1, bproj=1, b2_3=1, b1_3=4, g1=1, be1=1, g2=1, be2=1, cond=4)


def columns(widths):
    at, out = 0, {}
    for name, n in widths.items():
        out[name] = (at, at + n)
        at += n
    return out, at


W0_AT, W0_N = columns(W0_COLS)
W1_AT, W1_N = columns(W1_COLS)
W2_AT, W2_N = columns(W2_COLS)
W3_AT, W3_N = columns(W3_COLS)
VEC_AT, VEC_N = columns(VEC_COLS)

(SC0A, SH0A, G0A, GB0A, SC0B, SH0B, G0B, GB0B, SC2, SH2, G2, GB2,
 SC3A, SH3A, G3A, GB3A, SC3B, SH3B, G3B, GB3B) = range(20)
MODS = 20

GH = 4
GROUPS = H // GH
ST_LAG = GH + 2
PV_LAG = ST_LAG + 2
O_LAG = PV_LAG + 1
STEPS = H + O_LAG + 1
PT_RING = 3
EXP_LN_SET = "natural_log_exp_and_others"
GELU_SET = "gelu_and_others"
PARTS = 3
SLOTS = PARTS * PARTS
HEADS_PER_O = {0: 2, 2: 4, 3: 4}
EXP_SCALE = {0: float(DH0) ** -0.5, 2: 1.0, 3: float(DH) ** -0.5}
L1_UNITS = 2 * NT
L1_MASK, L1_MAX, L1_EXP, L1_SUM, L1_WEIGHTS, L1_TURN, L1_COPY, L1_Y, L1_ADD = 1, 2, 3, 4, 4, 5, 6, 7, 8
L1_LAG = L1_ADD

ATTENTIONS = [(layer, b) for layer in (0, 2, 3) for b in range(B)]
HEAVY = [phase for layer, b in ATTENTIONS for phase in ([("gv", b)] if layer == 0 else []) + [("attention", layer, b)]]


def before(layer, b):
    return [("norm", "0a", b)] if layer == 0 else [("norm", f"{layer}a", b), ("qkv", layer, b)]


def after(layer, b):
    return {0: [("norm", "0b", b), ("mlp", 0, b), ("layer1", b)], 2: [("norm", "2b", b)],
            3: [("norm", "3b", b), ("mlp", 3, b)]}[layer]


LIGHT = before(0, 0) + before(0, 1) + [("late mods",)] + [("edges", b) for b in range(B)]
for _n, _a in enumerate(ATTENTIONS):
    LIGHT += before(*ATTENTIONS[_n + ROOMS]) if _n + ROOMS < len(ATTENTIONS) else []
    LIGHT += [("project", *_a)] + after(*_a)
FM_TICK = 5
Y_TICK = 2
TICKS = {"late mods": 2, "norm": FM_TICK + 2, "edges": 8, "gv": H // 2 + 2 * NT + 1, "attention": 2 * STEPS,
         "project": 2, "mlp": Y_TICK + 2, "layer1": 7 + L1_UNITS + L1_LAG + 1, "qkv": 5}
STACK_TICKS = 18
EXTRA_EVERY = 4
U_BASE = {a: H * n for n, a in enumerate(ATTENTIONS)}
G_BASE = {a: GROUPS * n for n, a in enumerate(ATTENTIONS)}
O_BASE = {a: sum(H // HEADS_PER_O[x[0]] for x in ATTENTIONS[:n]) for n, a in enumerate(ATTENTIONS)}
NORMS = [p for p in LIGHT if p[0] == "norm"]
NORMS_TO_H = [p for p in NORMS if p[1] != "2b"]
X_UPDATES = [p for p in LIGHT if p[0] in ("project", "mlp", "layer1") or p[:2] == ("norm", "2b")]
QKVS = [p for p in LIGHT if p[0] == "qkv"]
MLPS = [p for p in LIGHT if p[0] == "mlp"]


def x_before(phase):
    earlier = [p for p in LIGHT[:LIGHT.index(phase)] if p in X_UPDATES and p[-1] == phase[-1]]
    return X_UPDATES.index(earlier[-1]) + 1 if earlier else 0


def x_after(*phase):
    return X_UPDATES.index(phase) + 1


def h_after(name, b):
    return NORMS_TO_H.index(("norm", name, b)) + 1


def mT_step_of(group):
    return GH * (group + 1) + 1


SCORE_TICKS = 2 * H - 1


def schedule():
    order, ticks, ended = [], {}, {}
    step = 0

    def tick(phase):
        order[-1][phase in LIGHT].append(phase)
        ticks[phase] = ticks.get(phase, 0) + 1
        if ticks[phase] == TICKS[phase[0]]:
            ended[phase] = step

    def can_start(phase):
        name, *args = phase
        if name == "gv":
            return ("norm", "0a", *args) in ended
        if name == "attention":
            layer, b = args
            n = ATTENTIONS.index((layer, b))
            if n >= ROOMS and ("project", *ATTENTIONS[n - ROOMS]) not in ended:
                return False
            if layer == 0:
                return ticks.get(("gv", b), 0) >= 2
            return ended.get(("qkv", layer, b), step) + STACK_TICKS <= step
        if name == "project":
            return ("attention", *args) in ended
        if name == "norm" and args[0] == "0a":
            return args[1] < H_ROOMS or ("attention", 0, args[1] - H_ROOMS) in ended
        if name == "qkv":
            return ticks.get(("attention", *ATTENTIONS[ATTENTIONS.index(tuple(args)) - ROOMS]), 0) > SCORE_TICKS
        return True

    while len(ended) < len(HEAVY) + len(LIGHT):
        order.append(([], []))
        last = None
        for phase in HEAVY:
            if phase not in ended and (phase in ticks or (can_start(phase) and (
                    last is None or last[0] == "gv" or ticks.get(last, 0) > SCORE_TICKS))):
                tick(phase)
            last = phase
        extra = step % EXTRA_EVERY == 0 and any(p[:2] == ("attention", 0) for p in order[-1][0])
        for _ in range(2 if extra else 1):
            phase = next((p for p in LIGHT if p not in ended), None)
            if phase and (phase in ticks or can_start(phase)):
                tick(phase)
        step += 1
    return order


def walk(phases, light_first=False):
    going = {}
    for heavy, light in SCHEDULE:
        for phase in light + heavy if light_first else heavy + light:
            if phase not in going:
                name, *args = phase
                going[phase] = phases[name](*args) if name in phases else iter(())
            next(going[phase], None)


def mT_step(i):
    return next((g for g in range(GROUPS) if mT_step_of(g) == i), None)


SCHEDULE = schedule()


def s_plan():
    plan = []

    def gv(b):
        for n in range(H // 2):
            plan.append(("G", n, b))
            yield
        for t in range(NT):
            for name in ("V by act", "V by dve"):
                plan.append((name, t, b))
                yield

    def attention(*a):
        for i in range(STEPS):
            if i < H:
                plan.append(("s", U_BASE[a] + i))
            yield
            if mT_step(i) is not None:
                plan.append(("mT", G_BASE[a] + mT_step(i)))
            yield

    walk(dict(gv=gv, attention=attention))
    return plan


S_PLAN = s_plan()
S_BANK_OF = {key: n % 2 for n, key in enumerate(S_PLAN)}


def o_at(layer, i):
    v, n = i - O_LAG, HEADS_PER_O[layer]
    return v // n if 0 <= v < H and v % n == n - 1 else None


def work_plan():
    plan = []

    def norm(name, b):
        plan.append(("tok", name, b))
        for _ in range(FM_TICK):
            yield
        plan.append(("fm", name, b))
        yield

    def late_mods():
        plan.extend([("mods",), ("qw",)])
        yield

    def project(layer, b):
        plan.append(("proj", layer, b))
        yield

    def mlp(layer, b):
        plan.extend(("ff", layer, c, b) for c in range(2))
        for _ in range(Y_TICK):
            yield
        plan.append(("y", layer, b))
        yield

    def layer1(b):
        plan.append(("nz", b))
        yield
        yield
        plan.append(("sf", b))
        yield
        yield
        plan.extend([("q1", b), ("k1", b)])
        yield
        plan.append(("v1", b))
        yield
        yield
        for i in range(L1_UNITS + L1_LAG):
            if 0 <= i - L1_Y < L1_UNITS:
                plan.append(("y1", i - L1_Y, b))
            if i < L1_UNITS:
                plan.append(("s1", i, b))
            if 0 <= i - L1_TURN < L1_UNITS:
                plan.append(("wT", i - L1_TURN, b))
            yield

    def qkv(layer, b):
        plan.extend([("qk", layer, b), ("v", layer, b)])
        yield

    walk({"late mods": late_mods} | dict(norm=norm, project=project, mlp=mlp, layer1=layer1, qkv=qkv))
    return {key: n for n, key in enumerate(plan)}


WORK = work_plan()


def cond_seq_kernel(nc, x_t, adj, w0, wqk0, w1, w2, w3, wp2, wproj3, vecs, rows, out_t):
    with ExitStack() as ctx:
        def sb(name, shape, dt=F32):
            return ctx.enter_context(nc.sbuf_tensor(name, shape, dt))

        def sem(name):
            return ctx.enter_context(nc.semaphore(name))

        w0s = sb("w0s", [128, W0_N])
        w1s = sb("w1s", [128, W1_N])
        w2s = sb("w2s", [128, W2_N])
        w3s = sb("w3s", [128, W3_N])
        wpad = {2: sb("wp2s", [128, 4, D]), 3: sb("wproj3s", [128, 4, D])}
        vec = sb("vec", [128, VEC_N])
        bv2 = sb("bv2", [128, D])
        wbias = sb("wbias", [128, NL + 1])
        a0 = sb("a0", [128, H, D])
        ident = sb("ident", [128, 128])
        identb = sb("identb", [128, 128], BF16)
        ones = sb("ones", [128, 64])
        eps = sb("eps", [128, 1])
        lnd = sb("lnd", [128, 1])
        zero = sb("zero", [128, 1])
        sel = sb("sel", [128, GH, 128], BF16)
        mask_qk = sb("mask_qk", [128, 128], BF16)
        mask_kq = sb("mask_kq", [128, 128], BF16)
        mask1 = sb("mask1", [128, H, NG])
        mask2 = sb("mask2", [128, 4, D])
        silu = sb("silu", [128, 3, B])
        raw = sb("raw", [128, 14, B])
        mods_all = sb("mods_all", [128, MODS, B])
        qw_all = sb("qw_all", [1, B, D])
        bq1s = sb("bq1s", [128, 2])
        bout1 = sb("bout1", [128, 1])

        xT = sb("xT", [128, B, T])
        xb = sb("xb", [128, B, T])
        keep1 = sb("keep1", [128, B, 2, NT * NG])
        bias1 = sb("bias1", [128, B, 2, NT * NG])
        hT0 = sb("hT0", [128, H_ROOMS, T])
        hTb = sb("hTb", [128, H_ROOMS, T], BF16)
        big = sb("big", [128, ROOMS, H * T])
        gT = big[:, :, :].rearrange("p r (h t) -> p r h t", h=H)
        stacks = big[:, :, :].bitcast(BF16).rearrange("p r (s h t) -> p r s h t", s=2, h=H)
        room = sb("room", [128, ROOMS, NT * H * DH0])
        wqk0s = room[0:DH0, :, :].rearrange("p s (h n) -> p s h n", h=H)
        v0 = room[:, :, :].rearrange("p r (t n) -> p r t n", t=NT)
        room3 = sb("room3", [128, ROOMS, H * T // 2])
        gTb = room3[:, :, :].bitcast(BF16).rearrange("p r (h t) -> p r h t", h=H)
        parts = room3[:, :, 0:3 * T].bitcast(BF16).rearrange("p r (n s t) -> p r n s t", s=2, n=PARTS)
        rest = room3[:, :, 3 * T:5 * T].rearrange("p r (s t) -> p r s t", s=2)
        oT = sb("oT", [128, ROOMS, 8, T])
        vpad = sb("vpad", [128, H_ROOMS, NT, H, 32])
        adj_s = sb("adj_s", [128, ROOMS, 2, NT, NG * NL], I32)
        hL = sb("hL", [128, T])
        stats = sb("stats", [128, NT, 6])
        mv = sb("mv", [128, NT, 2])
        lnv = sb("lnv", [128, NT])
        rstd = sb("rstd", [128, NT])
        xn = sb("xn", [128, NT, 128])
        room5 = sb("room5", [128, FC * T])
        ff = room5[:, :].rearrange("p (c t) -> p c t", c=FC)
        vbd = room5[:, :].rearrange("p (d c n) -> p d c n", d=2, c=4)
        wT = sb("wT", [128, 2, 4 * D])
        q1T = sb("q1T", [128, 2, T])
        kbd = sb("kbd", [128, 2, H * NG])
        sfT = sb("sfT", [128, T])
        sfb = sb("sfb", [128, T])
        sfrep = sb("sfrep", [128, 4, 32])
        nz = sb("nz", [1, T])
        cond1 = sb("cond1", [128, 2, NT * NG])
        vb1 = sb("vb1", [128, 2, NT * NG])
        room4 = sb("room4", [128, L1_UNITS * H * NG])
        aff = room4[:, :].rearrange("p (i h m) -> p i h m", i=L1_UNITS, h=H)
        adj_w = room4[:, 0:2 * NT * NG * NL].rearrange("p (d i l) -> p d i l", d=2, l=NL)
        negm = sb("negm", [128, 2, NT, GH])
        m2 = sb("m2", [128, 2, NT, 128], BF16)
        mT = sb("mT", [128, 2, T], BF16)
        pt = sb("pt", [128, PT_RING, NT * T])
        pairsum = sb("pairsum", [128, 2, T])
        rden = sb("rden", [128, 2, T])
        amax = sb("amax", [128, L1_UNITS, H])
        asum = sb("asum", [128, L1_UNITS, H])
        arec = sb("arec", [128, L1_UNITS, H])
        wgt = sb("wgt", [128, 2, H, 32])

        psum = ctx.enter_context(nc.psum_tensor("psum", [128, 8, 512], F32))
        S_BANK, ST_BANK, O_BANK, W_BANK = 0, 2, 4, 6
        scratch = nc.dram_tensor("scratch", [ROOMS, PARTS, 2, D, T], BF16).ap()

        first_in = sem("first_in")
        wqk_in = sem("wqk_in")
        weights_in = sem("weights_in")
        x_loaded = [sem(f"x_loaded{b}") for b in range(B)]
        pads_zero = sem("pads_zero")
        consts = sem("consts")
        consts_step = sem("consts_step")
        more_step = sem("more_step")
        more_consts = sem("more_consts")
        act_exp_c = sem("act_exp_c")
        silu_ready = sem("silu_ready")
        setup_step = sem("setup_step")
        mods_full = sem("mods_full")
        a0_full = sem("a0_full")
        a0_free = sem("a0_free")

        def col(at, name, i=0, n=1):
            return vec[:, VEC_AT[name][0] + i:VEC_AT[name][0] + i + n]

        with nc.Block() as block:
            @block.sync
            def _(sp):
                mod0 = slice(*W0_AT["mod"])
                sp.dma_start(vec[:], vecs).then_inc(first_in, 16)
                sp.dma_start(w0s[:, mod0], w0[:, mod0]).then_inc(first_in, 16)
                sp.dma_start(xT[:, 0, :], x_t[0]).then_inc(x_loaded[0], 16)
                sp.dma_start(wqk0s, wqk0).then_inc(wqk_in, 16)
                for b in range(1, B):
                    sp.dma_start(xT[:, b, :], x_t[b]).then_inc(x_loaded[b], 16)
                sp.dma_start(w0s[:, mod0.stop:], w0[:, mod0.stop:]).then_inc(weights_in, 16)
                sp.dma_start(wbias[:], rows[0:1, D:D + NL + 1].broadcast_to([128, NL + 1])).then_inc(weights_in, 16)
                sp.dma_start(w1s[:], w1).then_inc(weights_in, 16)
                sp.dma_start(w2s[:], w2).then_inc(weights_in, 16)
                sp.dma_start(w3s[:], w3).then_inc(weights_in, 16)
                sp.dma_start(bv2[:], rows[0:1, 0:D].broadcast_to([128, D])).then_inc(weights_in, 16)

            @block.gpsimd
            def _(pool):
                done = [0]

                def step(ins):
                    done[0] += 1
                    ins.then_inc(consts_step, 1)
                    pool.wait_ge(consts_step, done[0])

                step(nc.gpsimd.memset(ident[:], 0.0))
                step(nc.gpsimd.affine_select(out=ident[:], in_=ident[:], compare_op=ALU.not_equal, fill=1.0, base=0,
                                             pattern=[[-1, 128]], channel_multiplier=1))
                nc.gpsimd.tensor_copy(identb[:], ident[:]).then_inc(consts, 1)
                nc.gpsimd.memset(zero[:], 0.0)
                nc.gpsimd.memset(eps[:], EPS)
                nc.gpsimd.memset(lnd[:], -0.5 * math.log(D))
                nc.gpsimd.memset(ones[:], 1.0).then_inc(consts, 1)

            @block.scalar
            def _(act):
                act.wait_ge(first_in, 32)
                nc.scalar.activation(silu[:, 0, :], col(0, "cond", 0, B), ACT.Exp, scale=-1.0).then_inc(act_exp_c, 1)
                for n in range(4):
                    act.wait_ge(a0_full, n + 1)
                    nc.scalar.copy(a0[:, 4 * n:4 * n + 4, :], psum[:, n % 2, :]).then_inc(a0_free, 1)

            @block.vector
            def _(dve):
                done = [0]

                def step(ins):
                    done[0] += 1
                    ins.then_inc(setup_step, 1)
                    dve.wait_ge(setup_step, done[0])

                dve.wait_ge(first_in, 32)
                dve.wait_ge(act_exp_c, 1)
                step(nc.vector.tensor_scalar(silu[:, 1, :], silu[:, 0, :], 1.0, None, ALU.add))
                step(nc.vector.reciprocal(silu[:, 2, :], silu[:, 1, :]))
                nc.vector.tensor_tensor(silu[:, 0, :], silu[:, 2, :], col(0, "cond", 0, B), ALU.mult
                                        ).then_inc(silu_ready, 1)
                dve.wait_ge(mods_full, 1)
                step(nc.vector.tensor_tensor(raw[:, 0:6, :], psum[:, 2, 0:6 * B].rearrange("p (c b) -> p c b", b=B),
                                             col(0, "mods", 0, 6).unsqueeze(2).broadcast_to([128, 6, B]), ALU.add))

                def block_mods(base, sc, sh, gate, bias):
                    nc.vector.tensor_scalar(mods_all[:, base, :], raw[:, sc, :], 1.0, None, ALU.add)
                    nc.vector.tensor_copy(mods_all[:, base + 1, :], raw[:, sh, :])
                    nc.vector.tensor_copy(mods_all[:, base + 2, :], raw[:, gate, :])
                    step(nc.vector.tensor_scalar(mods_all[:, base + 3, :], raw[:, gate, :], bias, None, ALU.mult))

                block_mods(SC0A, 1, 0, 2, col(0, "b_out0"))
                block_mods(SC0B, 4, 3, 5, col(0, "b2_0"))
                nc.vector.tensor_scalar(bq1s[:], col(0, "bq1", 0, 2), float(DH) ** -0.5, None, ALU.mult)
                nc.vector.tensor_tensor(bout1[:], col(0, "bout1", 0), col(0, "bout1", 1), ALU.add)

            @block.tensor
            def _(pe):
                pe.wait_ge(first_in, 32)
                pe.wait_ge(silu_ready, 1)
                for c in range(6):
                    at = W0_AT["mod"][0] + D * c
                    mm = nc.tensor.matmul(psum[:, 2, B * c:B * c + B], w0s[:, at:at + D], silu[:, 0, :],
                                          start=True, stop=True)
                mm.then_inc(mods_full, 1)
                pe.wait_ge(wqk_in, 16)
                for n in range(4):
                    if n >= 2:
                        pe.wait_ge(a0_free, n - 1)
                    for h in range(4 * n, 4 * n + 4):
                        mm = nc.tensor.matmul(psum[:, n % 2, D * (h % 4):D * (h % 4) + D], wqk0s[:, 0, h, :],
                                              wqk0s[:, 1, h, :], start=True, stop=True)
                    mm.then_inc(a0_full, 1)

        pads_in = sem("pads_in")
        late_step = sem("late_step")
        work_full = [sem(f"work_full{i}") for i in range(2)]
        adj_loaded = [sem(f"adj_loaded{b}") for b in range(B)]
        stats_ready = sem("stats_ready")
        mv_ready = sem("mv_ready")
        lnv_ready = sem("lnv_ready")
        rstd_ready = sem("rstd_ready")
        xn_ready = sem("xn_ready")
        h_ready = sem("h_ready")
        xb_ready = sem("xb_ready")
        x_ready = sem("x_ready")
        ff_ready = sem("ff_ready")
        hb_ready = sem("hb_ready")
        g_full = sem("g_full")
        v_full = sem("v_full")
        g_ready = sem("g_ready")
        gb_ready = sem("gb_ready")
        v_by_act = sem("v_by_act")
        v_by_dve = sem("v_by_dve")
        vpad_ready = sem("vpad_ready")
        part1_ready = sem("part1_ready")
        rest_ready = sem("rest_ready")
        part2_ready = sem("part2_ready")
        part3_ready = sem("part3_ready")
        part_in_dram = [sem(f"part{p}_in_dram") for p in range(PARTS)]
        stack_zero = sem("stack_zero")
        stack_ready = sem("stack_ready")
        s_full = sem("s_full")
        max_done = sem("max_done")
        negm_hi = sem("negm_hi")
        m2_ready = sem("m2_ready")
        mT_full = sem("mT_full")
        mT_ready = sem("mT_ready")
        st_full = sem("st_full")
        pt_ready = sem("pt_ready")
        pairsum_ready = sem("pairsum_ready")
        pt_used = sem("pt_used")
        lnsum_ready = sem("lnsum_ready")
        rden_ready = sem("rden_ready")
        o_done = sem("o_done")
        adjw_ready = sem("adjw_ready")
        cond_step = sem("cond_step")
        nz_ready = sem("nz_ready")
        sf_ready = sem("sf_ready")
        sfrep_ready = sem("sfrep_ready")
        q1_ready = sem("q1_ready")
        kbd_ready = sem("kbd_ready")
        vbd_ready = sem("vbd_ready")
        aff_masked = sem("aff_masked")
        aff_biased = sem("aff_biased")
        amax_ready = sem("amax_ready")
        aff_shifted = sem("aff_shifted")
        aff_exp = sem("aff_exp")
        asum_ready = sem("asum_ready")
        arec_ready = sem("arec_ready")
        wgt_ready = sem("wgt_ready")
        wT_ready = sem("wT_ready")
        y1_sum = sem("y1_sum")
        out_stored = sem("out_stored")

        def slot(key):
            return WORK[key] % 2

        def bank(key):
            return psum[:, W_BANK + slot(key), :]

        def wait_full(eng, key):
            eng.wait_ge(work_full[slot(key)], WORK[key] // 2 + 1)

        read_by = {}
        in_order = list(WORK)

        def wait_free(pe, key):
            if WORK[key] >= 2:
                signal, value = read_by[in_order[WORK[key] - 2]]
                pe.wait_ge(signal, value)

        def s_bank(*key):
            return psum[:, S_BANK + S_BANK_OF[key], :]

        def wait_s_bank_free(pe, *key):
            at = S_PLAN.index(key)
            if at >= 2:
                kind, n, *b = S_PLAN[at - 2]
                reader, of_batch = {"s": (max_done, 0), "mT": (mT_ready, 0), "G": (g_ready, H // 2),
                                    "V by act": (v_by_act, NT), "V by dve": (v_by_dve, NT)}[kind]
                pe.wait_ge(reader, n + 1 + (of_batch * b[0] if b else 0))

        def mod(i, b):
            return mods_all[:, i, b:b + 1]

        with nc.Block() as block:
            @block.sync
            def _(sp):
                for b in range(B):
                    if b >= ROOMS:
                        sp.wait_ge(cond_step, 7 * (b - ROOMS) + 4)
                    for n in range(NT):
                        nodes = slice(n * 128, (n + 1) * 128)
                        sp.dma_start(adj_s[:, b % ROOMS, 0, n, :].rearrange("p (m l) -> p m l", l=NL),
                                     adj[b, nodes, 0:NG, :]).then_inc(adj_loaded[b], 16)
                        sp.dma_start(adj_s[:, b % ROOMS, 1, n, :].rearrange("p (m l) -> p m l", l=NL),
                                     adj[b, 0:NG, nodes, :].rearrange("m p l -> p m l")).then_inc(adj_loaded[b], 16)
                sp.wait_ge(pads_zero, 2)
                for src, dst in ((wp2, wpad[2]), (wproj3, wpad[3])):
                    by_j = src.rearrange("(g j d) n -> j d g n", g=4, j=4)
                    for j in range(4):
                        sp.dma_start(dst[32 * j:32 * j + DH, :, :], by_j[j]).then_inc(pads_in, 16)
                for a, (_, layer, b) in enumerate(QKVS):
                    r = b % ROOMS
                    if a >= ROOMS:
                        sp.wait_ge(stack_ready, 16 * 2 * SLOTS * (a - ROOMS + 1))
                    for p in range(PARTS):
                        sp.wait_ge((part1_ready, part2_ready, part3_ready)[p], (2, 1, 1)[p] * (a + 1))
                        sp.dma_start(scratch[r, p].rearrange("s f t -> f s t"), parts[:, r, p]
                                     ).then_inc(part_in_dram[p], 16)
                    sp.wait_ge(st_full, U_BASE[ATTENTIONS[B + a - ROOMS]] + H)
                    if a < ROOMS:
                        sp.wait_ge(stack_zero, 4 * (a + 1))
                    for p in range(PARTS):
                        sp.wait_ge(part_in_dram[p], 16 * (a + 1))
                        for s in range(2):
                            by_head = scratch[r, p, s].rearrange("(h d) t -> d h t", d=DH)
                            for o in range(PARTS):
                                n = PARTS * p + o if s == 0 else PARTS * o + p
                                sp.dma_start(stacks[DH * n:DH * n + DH, r, s], by_head).then_inc(stack_ready, 16)
                for b in range(B):
                    sp.wait_ge(x_ready, x_after("mlp", 3, b))
                    sp.dma_start(out_t[b], xT[:, b, :]).then_inc(out_stored, 16)
                sp.wait_ge(out_stored, 16 * B)

            @block.gpsimd
            def _(pool):
                zeros = [0]
                latest = {}

                def attention(layer, b):
                    q0 = 128 if layer == 3 else 0
                    for i in range(STEPS):
                        yield
                        if 0 <= i - ST_LAG < H:
                            u = U_BASE[layer, b] + i - ST_LAG
                            pool.wait_ge(pt_ready, u + 1)
                            if u >= 2:
                                pool.wait_ge(pt_used, u - 1)
                            nc.gpsimd.tensor_tensor(pairsum[:, u % 2, q0:T], pt[:, u % PT_RING, q0:T],
                                                    pt[:, u % PT_RING, T:2 * T - q0], ALU.add
                                                    ).then_inc(pairsum_ready, 1)
                            latest[pairsum_ready] = u + 1
                        n = i - H - ST_LAG
                        if layer == 0 and b >= B - ROOMS and n >= 0:
                            for signal, value in latest.items():
                                pool.wait_ge(signal, value)
                            if n == 0:
                                pool.wait_ge(st_full, U_BASE[layer, b] + H)
                            nc.gpsimd.memset(big[64:128, b % ROOMS, n * H * T // 4:(n + 1) * H * T // 4], 0.0
                                             ).then_inc(stack_zero, 1)
                            zeros[0] += 1
                            pool.wait_ge(stack_zero, zeros[0])
                        yield

                def layer1(b):
                    first = L1_UNITS * b
                    for _ in range(7):
                        yield
                    for tick in range(L1_UNITS + L1_LAG):
                        i = tick - L1_MASK
                        if 0 <= i < L1_UNITS:
                            pool.wait_ge(aff_masked, first + i + 1)
                            if i == 0:
                                pool.wait_ge(cond_step, 7 * (b + 1))
                            t, d = i // 2, i % 2
                            bias = bias1[:, b, d, t * NG:(t + 1) * NG].unsqueeze(1).broadcast_to([128, H, NG])
                            nc.gpsimd.tensor_tensor(aff[:, i], aff[:, i], bias, ALU.add).then_inc(aff_biased, 1)
                            latest[aff_biased] = first + i + 1
                        w = tick - L1_MAX
                        if 0 <= w < L1_UNITS:
                            pool.wait_ge(amax_ready, first + w + 1)
                            pool.wait_ge(aff_biased, first + w + 1)
                            nc.gpsimd.tensor_tensor(aff[:, w], aff[:, w],
                                                    amax[:, w, :].unsqueeze(2).broadcast_to([128, H, NG]),
                                                    ALU.subtract).then_inc(aff_shifted, 1)
                            latest[aff_shifted] = first + w + 1
                        w = tick - L1_WEIGHTS
                        if 0 <= w < L1_UNITS:
                            pool.wait_ge(arec_ready, first + w + 1)
                            if w >= 2:
                                wait_full(pool, ("wT", w - 2, b))
                            nc.gpsimd.tensor_tensor(wgt[:, w % 2, :, 0:NG], aff[:, w],
                                                    arec[:, w, :].unsqueeze(2).broadcast_to([128, H, NG]),
                                                    ALU.mult).then_inc(wgt_ready, 1)
                            latest[wgt_ready] = first + w + 1
                        yield

                def norm(name, b):
                    for _ in range(3):
                        yield
                    gb = {"0a": GB0A, "0b": GB0B, "2a": GB2, "2b": SH2, "3a": GB3A, "3b": GB3B}[name]
                    updates = x_before(("norm", name, b))
                    if updates:
                        pool.wait_ge(x_ready, updates)
                    else:
                        pool.wait_ge(x_loaded[b], 16)
                    nc.gpsimd.tensor_scalar(xb[:, b], xT[:, b], mod(gb, b), None, ALU.add).then_inc(xb_ready, 1)
                    latest[xb_ready] = NORMS.index(("norm", name, b)) + 1

                done = [0]

                def step(ins):
                    done[0] += 1
                    ins.then_inc(more_step, 1)
                    pool.wait_ge(more_step, done[0])

                step(nc.gpsimd.memset(sel[:], 0.0))
                for part in range(2):
                    step(nc.gpsimd.affine_select(out=sel[:], in_=sel[:], compare_op=ALU.not_equal, fill=1.0,
                                                 base=-GH * part, pattern=[[-1, GH], [0, 128]], channel_multiplier=1))
                step(nc.gpsimd.memset(mask_qk[:], 0.0))
                step(nc.gpsimd.memset(mask_kq[:], 0.0))
                step(nc.gpsimd.affine_select(out=mask_qk[:], in_=mask_qk[:], compare_op=ALU.is_ge, fill=MASKED, base=0,
                                             pattern=[[-1, 128]], channel_multiplier=1))
                step(nc.gpsimd.affine_select(out=mask_kq[:], in_=mask_kq[:], compare_op=ALU.is_ge, fill=MASKED, base=0,
                                             pattern=[[1, 128]], channel_multiplier=-1))
                step(nc.gpsimd.memset(mask1[:], 1.0))
                step(nc.gpsimd.affine_select(out=mask1[:], in_=mask1[:], compare_op=ALU.is_ge, fill=0.0, base=0,
                                             pattern=[[-DH, H], [0, NG]], channel_multiplier=1))
                step(nc.gpsimd.affine_select(out=mask1[:], in_=mask1[:], compare_op=ALU.is_ge, fill=0.0, base=DH - 1,
                                             pattern=[[DH, H], [0, NG]], channel_multiplier=-1))
                m2v = mask2[:, :, :].rearrange("p c (h g) -> p c h g", g=DH)
                step(nc.gpsimd.memset(mask2[:], 1.0))
                step(nc.gpsimd.affine_select(out=m2v, in_=m2v, compare_op=ALU.is_ge, fill=0.0, base=0,
                                             pattern=[[128, 4], [-32, H], [0, DH]], channel_multiplier=1))
                step(nc.gpsimd.affine_select(out=m2v, in_=m2v, compare_op=ALU.is_ge, fill=0.0, base=31,
                                             pattern=[[-128, 4], [32, H], [0, DH]], channel_multiplier=-1))
                nc.gpsimd.memset(m2[:], 0.0)
                nc.gpsimd.memset(vpad[:], 0.0)
                nc.gpsimd.memset(sfrep[:], 0.0)
                nc.gpsimd.memset(wgt[:], 0.0).then_inc(more_consts, 1)
                nc.gpsimd.memset(wpad[2][:], 0.0).then_inc(pads_zero, 1)
                nc.gpsimd.memset(wpad[3][:], 0.0).then_inc(pads_zero, 1)
                walk(dict(attention=attention, norm=norm, layer1=layer1), light_first=True)

            @block.scalar
            def _(act):
                def norm(name, b):
                    n = NORMS.index(("norm", name, b))
                    yield
                    yield
                    act.wait_ge(mv_ready, NT * (n + 1))
                    nc.scalar.activation(lnv[:], mv[:, :, 1], ACT.Ln, bias=eps[:, 0:1]
                                         ).then_inc(lnv_ready, 1)
                    act.wait_ge(lnv_ready, n + 1)
                    nc.scalar.activation(rstd[:], lnv[:], ACT.Exp, scale=-0.5).then_inc(rstd_ready, 1)
                    if name == "2b":
                        return
                    for _ in range(FM_TICK - 1):
                        yield
                    fm, sc = ("fm", name, b), {"0a": SC0A, "0b": SC0B, "2a": SC2, "3a": SC3A, "3b": SC3B}[name]
                    wait_full(act, fm)
                    if name == "0a" and b >= H_ROOMS:
                        act.wait_ge(st_full, U_BASE[0, b - H_ROOMS] + H)
                    nc.scalar.activation(hT0[:, b % H_ROOMS] if name == "0a" else hL[:], bank(fm)[:, 0:T], ACT.Identity,
                                         scale=mod(sc, b), bias=mod(sc + 1, b)).then_inc(h_ready, 1)
                    read_by[fm] = (h_ready, h_after(name, b))

                def gv(b):
                    act.wait_ge(h_ready, h_after("0a", b))
                    nc.scalar.copy(hTb[:, b % H_ROOMS], hT0[:, b % H_ROOMS]).then_inc(hb_ready, 1)
                    for n in range(H // 2):
                        yield
                        act.wait_ge(g_ready, H // 2 * b + n + 1)
                        nc.scalar.copy(gTb[:, b % ROOMS, 2 * n:2 * n + 2], gT[:, b % ROOMS, 2 * n:2 * n + 2]
                                       ).then_inc(gb_ready, 1)
                    for t in range(NT):
                        if b >= ROOMS:
                            act.wait_ge(pt_used, U_BASE[0, b - ROOMS] + H)
                        act.wait_ge(v_full, 2 * (NT * b + t) + 1)
                        nc.scalar.copy(v0[:, b % ROOMS, t, 0:512], s_bank("V by act", t, b)).then_inc(v_by_act, 1)
                        yield
                        yield

                def attention(layer, b):
                    width = NT * T if layer != 3 else T + 128
                    for i in range(STEPS):
                        yield
                        g = mT_step(i)
                        if g is not None:
                            at = G_BASE[layer, b] + g
                            act.wait_ge(mT_full, at + 1)
                            nc.scalar.copy(mT[:, at % 2, :], s_bank("mT", at)[:, 0:T // 2].bitcast(BF16)
                                           ).then_inc(mT_ready, 1)
                        if 0 <= i - ST_LAG < H:
                            u = U_BASE[layer, b] + i - ST_LAG
                            act.wait_ge(st_full, u + 1)
                            if u >= PT_RING:
                                act.wait_ge(pt_used, u - PT_RING + 1)
                            nc.scalar.activation(pt[:, u % PT_RING, 0:width], psum[:, ST_BANK + u % 2, 0:width],
                                                 ACT.Exp, scale=EXP_SCALE[layer]).then_inc(pt_ready, 1)
                        o = o_at(layer, i)
                        if o is not None:
                            o += O_BASE[layer, b]
                            act.wait_ge(pt_used, U_BASE[layer, b] + i - O_LAG + 1)
                            if o >= 2:
                                act.wait_ge(o_done, o - 1)
                            nc.scalar.activation(rden[:, o % 2, :], psum[:, O_BANK + o % 2, T:2 * T],
                                                 ACT.Ln).then_inc(lnsum_ready, 1)
                            act.wait_ge(lnsum_ready, o + 1)
                            nc.scalar.activation(rden[:, o % 2, :], rden[:, o % 2, :], ACT.Exp, scale=-1.0,
                                                 bias=(lnd if layer == 2 else zero)[:, 0:1]).then_inc(rden_ready, 1)
                        yield

                def mlp(layer, b):
                    yield
                    nc.scalar.preload_act_table_set(GELU_SET)
                    for c in range(FC):
                        key = ("ff", layer, c // 2, b)
                        wait_full(act, key)
                        done = FC * MLPS.index(("mlp", layer, b)) + c + 1
                        nc.scalar.activation(ff[:, c, :], bank(key)[:, (c % 2) * T:(c % 2 + 1) * T], ACT.Gelu,
                                             bias=col(0, "b1_0" if layer == 0 else "b1_3", c)
                                             ).then_inc(ff_ready, 1)
                        read_by[key] = (ff_ready, done)
                    nc.scalar.preload_act_table_set(EXP_LN_SET)

                def layer1(b):
                    first = L1_UNITS * b
                    for _ in range(3):
                        yield
                    wait_full(act, ("sf", b))
                    nc.scalar.activation(sfT[:], bank(("sf", b))[:, 0:T], ACT.Identity, bias=col(0, "b_self")
                                         ).then_inc(sf_ready, 1)
                    read_by["sf", b] = (sf_ready, b + 1)
                    yield
                    yield
                    wait_full(act, ("q1", b))
                    for d in range(2):
                        nc.scalar.activation(q1T[:, d], bank(("q1", b))[:, d * T:(d + 1) * T], ACT.Identity,
                                             bias=bq1s[:, d:d + 1], scale=float(DH) ** -0.5
                                             ).then_inc(q1_ready, 1)
                    read_by["q1", b] = (q1_ready, 2 * (b + 1))
                    yield
                    yield
                    for tick in range(L1_UNITS + L1_LAG):
                        w = tick - L1_EXP
                        if 0 <= w < L1_UNITS:
                            act.wait_ge(aff_shifted, first + w + 1)
                            nc.scalar.activation(aff[:, w], aff[:, w], ACT.Exp).then_inc(aff_exp, 1)
                        w = tick - L1_COPY
                        if 0 <= w < L1_UNITS:
                            key = ("wT", w, b)
                            wait_full(act, key)
                            if w >= 2:
                                wait_full(act, ("y1", w - 2, b))
                            nc.scalar.copy(wT[:, w % 2, :], bank(key)).then_inc(wT_ready, 1)
                            read_by[key] = (wT_ready, first + w + 1)
                        yield

                def qkv(layer, b):
                    a = QKVS.index(("qkv", layer, b))
                    yield
                    act.wait_ge(s_full, U_BASE[ATTENTIONS[B + a - ROOMS]] + H)
                    if a >= ROOMS:
                        for p in range(PARTS):
                            act.wait_ge(part_in_dram[p], 16 * (a - ROOMS + 1))
                    key = ("qk", layer, b)
                    wait_full(act, key)
                    for s, name in enumerate("qk"):
                        nc.scalar.activation(parts[:, b % ROOMS, 0, s], bank(key)[:, s * T:(s + 1) * T], ACT.Identity,
                                             bias=col(0, f"b{name}2") if layer == 2 else zero[:, 0:1]
                                             ).then_inc(part1_ready, 1)
                    yield
                    yield
                    act.wait_ge(rest_ready, 2 * (a + 1))
                    nc.scalar.copy(parts[:, b % ROOMS, 1], rest[:, b % ROOMS]).then_inc(part2_ready, 1)

                nc.scalar.preload_act_table_set(EXP_LN_SET)
                walk(dict(norm=norm, gv=gv, attention=attention, mlp=mlp, layer1=layer1, qkv=qkv), light_first=True)

            @block.vector
            def _(dve):
                xb_at = [0] * B

                def gated(key, b, gate, x_updates):
                    wait_full(dve, key)
                    dve.wait_ge(xb_ready, xb_at[b])
                    nc.vector.scalar_tensor_tensor(out=xT[:, b], in0=bank(key)[:, 0:T], scalar=mod(gate, b),
                                                   in1=xb[:, b], op0=ALU.mult, op1=ALU.add
                                                   ).then_inc(x_ready, 1)
                    read_by[key] = (x_ready, x_updates)

                def norm(name, b):
                    sc = {"0a": SC0A, "0b": SC0B, "2a": SC2, "2b": SC2, "3a": SC3A, "3b": SC3B}[name]
                    n = NORMS.index(("norm", name, b))
                    tok, fm = ("tok", name, b), ("fm", name, b)
                    yield
                    wait_full(dve, tok)
                    for t in range(NT):
                        nc.vector.bn_stats(stats[:, t, :], bank(tok)[:, t * 128:(t + 1) * 128]
                                           ).then_inc(stats_ready, 1)
                    for t in range(NT):
                        dve.wait_ge(stats_ready, NT * n + t + 1)
                        nc.vector.bn_aggr(mv[:, t, :], stats[:, t, :]).then_inc(mv_ready, 1)
                    yield
                    yield
                    dve.wait_ge(rstd_ready, n + 1)
                    dve.wait_ge(mv_ready, NT * (n + 1))
                    for t in range(NT):
                        nc.vector.tensor_scalar(xn[:, t, :], bank(tok)[:, t * 128:(t + 1) * 128],
                                                mv[:, t, 0:1], rstd[:, t:t + 1], ALU.subtract, ALU.mult
                                                ).then_inc(xn_ready, 1)
                    read_by[tok] = (xn_ready, NT * (n + 1))
                    xb_at[b] = n + 1
                    for _ in range(FM_TICK - 2):
                        yield
                    wait_full(dve, fm)
                    if name == "2b":
                        dve.wait_ge(xb_ready, xb_at[b])
                        nc.vector.scalar_tensor_tensor(out=xT[:, b], in0=bank(fm)[:, 0:T], scalar=mod(sc, b),
                                                       in1=xb[:, b], op0=ALU.mult, op1=ALU.add
                                                       ).then_inc(x_ready, 1)
                        read_by[fm] = (x_ready, x_after("norm", "2b", b))
                    yield

                def gv(b):
                    for n in range(H // 2):
                        if b >= ROOMS and n == 0:
                            dve.wait_ge(st_full, U_BASE[0, b - ROOMS] + H)
                        dve.wait_ge(g_full, H // 2 * b + n + 1)
                        nc.vector.tensor_copy(gT[:, b % ROOMS, 2 * n:2 * n + 2], s_bank("G", n, b).rearrange(
                            "p (h t) -> p h t", h=2)).then_inc(g_ready, 1)
                        yield
                    for t in range(NT):
                        yield
                        if b >= ROOMS:
                            dve.wait_ge(pt_used, U_BASE[0, b - ROOMS] + H)
                        dve.wait_ge(v_full, 2 * (NT * b + t) + 2)
                        nc.vector.tensor_copy(v0[:, b % ROOMS, t, 512:1024], s_bank("V by dve", t, b)
                                              ).then_inc(v_by_dve, 1)
                        yield

                def attention(layer, b):
                    for i in range(STEPS):
                        if i < H:
                            u = U_BASE[layer, b] + i
                            at = G_BASE[layer, b] + i // GH
                            g, j = at % 2, i % GH
                            bk = s_bank("s", u)
                            dve.wait_ge(s_full, u + 1)
                            if layer == 3:
                                nc.vector.tensor_reduce(negm[:, g, 0, j:j + 1], bk[:, 0:128], AX_X, ALU.max,
                                                        negate=True)
                                ins = nc.vector.tensor_reduce(negm[:, g, 1, j:j + 1], bk[:, 128:384], AX_X,
                                                              ALU.max, negate=True)
                            else:
                                ins = nc.vector.tensor_reduce(negm[:, g, :, j], bk.rearrange("p (q k) -> p q k", q=NT),
                                                              AX_X, ALU.max, negate=True)
                            ins.then_inc(max_done, 1)
                            if j == GH - 1:
                                dve.wait_ge(max_done, u + 1)
                                if at >= 2:
                                    dve.wait_ge(mT_full, at - 1)
                                if at == 0:
                                    dve.wait_ge(more_consts, 1)
                                hi, lo = m2[:, g, :, 0:GH], m2[:, g, :, GH:2 * GH]
                                nc.vector.tensor_copy(hi, negm[:, g]).then_inc(negm_hi, 1)
                                dve.wait_ge(negm_hi, at + 1)
                                nc.vector.tensor_tensor(lo, negm[:, g], hi, ALU.subtract).then_inc(m2_ready, 1)
                        yield
                        o = o_at(layer, i - 1)
                        if o is not None:
                            c = o
                            o += O_BASE[layer, b]
                            dve.wait_ge(rden_ready, o + 1)
                            nc.vector.tensor_tensor(oT[:, b % ROOMS, c, :], psum[:, O_BANK + o % 2, 0:T],
                                                    rden[:, o % 2, :], ALU.mult).then_inc(o_done, 1)
                        yield

                def project(layer, b):
                    yield
                    gated(("proj", layer, b), b, {0: G0A, 2: G2, 3: G3A}[layer], x_after("project", layer, b))

                def mlp(layer, b):
                    for _ in range(Y_TICK + 1):
                        yield
                    gated(("y", layer, b), b, {0: G0B, 3: G3B}[layer], x_after("mlp", layer, b))

                def late_mods():
                    yield
                    done = [0]

                    def step(ins):
                        done[0] += 1
                        ins.then_inc(late_step, 1)
                        dve.wait_ge(late_step, done[0])

                    wait_full(dve, ("mods",))
                    step(nc.vector.tensor_tensor(raw[:, 6:14, :], bank(("mods",))[:, 0:8 * B].rearrange(
                        "p (c b) -> p c b", b=B), col(0, "mods", 6, 8).unsqueeze(2).broadcast_to([128, 8, B]), ALU.add))
                    read_by["mods",] = (late_step, 1)

                    def mod4(i):
                        return mods_all[:, i, :]

                    for base, sc, sh, gate, bias in ((SC3A, 7, 6, 8, "bproj"), (SC3B, 10, 9, 11, "b2_3")):
                        nc.vector.tensor_scalar(mod4(base), raw[:, sc, :], 1.0, None, ALU.add)
                        nc.vector.tensor_copy(mod4(base + 1), raw[:, sh, :])
                        nc.vector.tensor_copy(mod4(base + 2), raw[:, gate, :])
                        step(nc.vector.tensor_scalar(mod4(base + 3), raw[:, gate, :], col(0, bias), None, ALU.mult))
                    for sc, gain, be in ((SC3A, "g1", "be1"), (SC3B, "g2", "be2")):
                        step(nc.vector.scalar_tensor_tensor(out=mod4(sc + 1), in0=mod4(sc), scalar=col(0, be),
                                                            in1=mod4(sc + 1), op0=ALU.mult, op1=ALU.add))
                        step(nc.vector.tensor_scalar(mod4(sc), mod4(sc), col(0, gain), None, ALU.mult))
                    nc.vector.tensor_scalar(mod4(SC2), raw[:, 12, :], col(0, "ln_g"), None, ALU.mult)
                    nc.vector.scalar_tensor_tensor(out=mod4(SH2), in0=raw[:, 12, :], scalar=col(0, "ln_b"),
                                                   in1=raw[:, 13, :], op0=ALU.mult, op1=ALU.add)
                    step(nc.vector.memset(mod4(G2), 1.0))
                    step(nc.vector.tensor_scalar(mod4(GB2), mod4(G2), col(0, "bp"), None, ALU.mult))
                    wait_full(dve, ("qw",))
                    step(nc.vector.tensor_copy(qw_all[:], bank(("qw",))[0:1, 0:B * D]))
                    read_by["qw",] = (late_step, done[0])

                def edges(b):
                    adj_m = [adj_s[:, b % ROOMS, d].rearrange("p i (m l) -> p (i m) l", l=NL) for d in range(2)]
                    wb = wbias[:, 0:NL].unsqueeze(1).broadcast_to([128, NT * NG, NL])
                    dve.wait_ge(weights_in, 16 * 6)
                    dve.wait_ge(adj_loaded[b], 16 * 2 * NT)
                    if b:
                        dve.wait_ge(cond_step, 7 * b)
                    for d in range(2):
                        yield
                        nc.vector.tensor_tensor(adj_w[:, d], adj_m[d], wb, ALU.mult).then_inc(adjw_ready, 1)
                    for d in range(2):
                        yield
                        nc.vector.tensor_reduce(cond1[:, d], adj_m[d], AX_X, ALU.add).then_inc(cond_step, 1)
                    for d in range(2):
                        yield
                        dve.wait_ge(adjw_ready, 2 * b + d + 1)
                        nc.vector.tensor_reduce(vb1[:, d], adj_w[:, d], AX_X, ALU.add).then_inc(cond_step, 1)
                    yield
                    dve.wait_ge(cond_step, 7 * b + 4)
                    nc.vector.tensor_scalar(keep1[:, b], cond1[:], 0.0, None, ALU.is_gt).then_inc(cond_step, 1)
                    dve.wait_ge(cond_step, 7 * b + 5)
                    nc.vector.tensor_scalar(cond1[:], keep1[:, b], 1.0, -NEG, ALU.subtract, ALU.mult
                                            ).then_inc(cond_step, 1)
                    dve.wait_ge(cond_step, 7 * b + 6)
                    nc.vector.scalar_tensor_tensor(out=bias1[:, b], in0=vb1[:], scalar=wbias[:, NL:NL + 1],
                                                   in1=cond1[:], op0=ALU.add, op1=ALU.add
                                                   ).then_inc(cond_step, 1)
                    yield

                def layer1(b):
                    first = L1_UNITS * b
                    yield
                    wait_full(dve, ("nz", b))
                    nc.vector.tensor_scalar(nz[:], bank(("nz", b))[0:1, 0:T], 0.0, None, ALU.not_equal
                                            ).then_inc(nz_ready, 1)
                    read_by["nz", b] = (nz_ready, b + 1)
                    yield
                    yield
                    yield
                    dve.wait_ge(sf_ready, b + 1)
                    nc.vector.tensor_copy(sfrep[:, :, 0:NG],
                                          sfT[:, 0:NG].unsqueeze(1).broadcast_to([128, 4, NG])
                                          ).then_inc(sfrep_ready, 1)
                    nc.vector.tensor_scalar(sfb[:], sfT[:], bout1[:, 0:1], None, ALU.add
                                            ).then_inc(sfrep_ready, 1)
                    yield
                    wait_full(dve, ("k1", b))
                    for d in range(2):
                        src = bank(("k1", b))[:, d * NG:(d + 1) * NG].unsqueeze(1)
                        nc.vector.scalar_tensor_tensor(out=kbd[:, d].rearrange("p (h m) -> p h m", h=H),
                                                       in0=src.broadcast_to([128, H, NG]), scalar=col(0, "bk1", d),
                                                       in1=mask1[:], op0=ALU.add, op1=ALU.mult
                                                       ).then_inc(kbd_ready, 1)
                    read_by["k1", b] = (kbd_ready, 2 * (b + 1))
                    yield
                    wait_full(dve, ("v1", b))
                    for d in range(2):
                        src = bank(("v1", b))[:, d * D:(d + 1) * D].unsqueeze(1)
                        nc.vector.tensor_tensor(vbd[:, d], src.broadcast_to([128, 4, D]), mask2[:], ALU.mult
                                                ).then_inc(vbd_ready, 1)
                    read_by["v1", b] = (vbd_ready, 2 * (b + 1))
                    yield
                    for tick in range(L1_UNITS + L1_LAG):
                        w = tick - L1_ADD
                        if 0 <= w < L1_UNITS:
                            key, t = ("y1", w, b), w // 2
                            wait_full(dve, key)
                            if w < 2:
                                dve.wait_ge(sfrep_ready, 2 * (b + 1))
                            if w:
                                dve.wait_ge(y1_sum, first + w)
                            nc.vector.tensor_tensor(sfb[:, t * 128:(t + 1) * 128], bank(key)[:, 0:128],
                                                    sfb[:, t * 128:(t + 1) * 128], ALU.add).then_inc(y1_sum, 1)
                            read_by[key] = (y1_sum, first + w + 1)
                        i = tick - L1_MASK
                        if 0 <= i < L1_UNITS:
                            t, d = i // 2, i % 2
                            wait_full(dve, ("s1", i, b))
                            keep = keep1[:, b, d, t * NG:(t + 1) * NG].unsqueeze(1).broadcast_to([128, H, NG])
                            nc.vector.tensor_tensor(aff[:, i], bank(("s1", i, b))[:, 0:H * NG].rearrange(
                                "p (h m) -> p h m", h=H), keep, ALU.mult).then_inc(aff_masked, 1)
                            read_by["s1", i, b] = (aff_masked, first + i + 1)
                        w = tick - L1_MAX
                        if 0 <= w < L1_UNITS:
                            dve.wait_ge(aff_biased, first + w + 1)
                            nc.vector.tensor_reduce(amax[:, w, :], aff[:, w], AX_X, ALU.max).then_inc(amax_ready, 1)
                        w = tick - L1_SUM
                        if 0 <= w < L1_UNITS:
                            dve.wait_ge(aff_exp, first + w + 1)
                            nc.vector.tensor_reduce(asum[:, w, :], aff[:, w], AX_X, ALU.add).then_inc(asum_ready, 1)
                            dve.wait_ge(asum_ready, first + w + 1)
                            nc.vector.reciprocal(arec[:, w, :], asum[:, w, :]).then_inc(arec_ready, 1)
                        yield
                    dve.wait_ge(y1_sum, first + L1_UNITS)
                    nc.vector.scalar_tensor_tensor(out=xT[:, b], in0=sfb[:], scalar=0.0, in1=xT[:, b],
                                                   op0=ALU.max, op1=ALU.add).then_inc(x_ready, 1)

                def qkv(layer, b):
                    a = QKVS.index(("qkv", layer, b))
                    qk, v = ("qk", layer, b), ("v", layer, b)
                    yield
                    yield
                    dve.wait_ge(part1_ready, 2 * (a + 1))
                    for s, name in enumerate("qk"):
                        nc.vector.scalar_tensor_tensor(out=rest[:, b % ROOMS, s], in0=bank(qk)[:, s * T:(s + 1) * T],
                                                       scalar=col(0, f"b{name}2") if layer == 2 else zero[:, 0:1],
                                                       in1=parts[:, b % ROOMS, 0, s], op0=ALU.add, op1=ALU.subtract
                                                       ).then_inc(rest_ready, 1)
                    read_by[qk] = (rest_ready, 2 * (a + 1))
                    wait_full(dve, v)
                    vroom = a % H_ROOMS
                    if a >= H_ROOMS:
                        dve.wait_ge(pt_used, U_BASE[ATTENTIONS[B + a - H_ROOMS]] + H)
                    for t in range(NT):
                        src = bank(v)[:, t * D:(t + 1) * D].rearrange("p (h d) -> p h d", h=H)
                        if layer == 2:
                            ins = nc.vector.tensor_tensor(vpad[:, vroom, t, :, 0:DH], src,
                                                          bv2[:, :].rearrange("p (h d) -> p h d", h=H), ALU.add)
                        else:
                            ins = nc.vector.tensor_copy(vpad[:, vroom, t, :, 0:DH], src)
                        ins.then_inc(vpad_ready, 1)
                    read_by[v] = (vpad_ready, NT * (a + 1))
                    yield
                    yield
                    dve.wait_ge(part2_ready, a + 1)
                    nc.vector.tensor_tensor(parts[:, b % ROOMS, 2], rest[:, b % ROOMS], parts[:, b % ROOMS, 1], ALU.subtract
                                            ).then_inc(part3_ready, 1)

                walk({"late mods": late_mods} | dict(norm=norm, gv=gv, attention=attention, project=project, mlp=mlp,
                                                      edges=edges,
                          layer1=layer1, qkv=qkv), light_first=True)

            @block.tensor
            def _(pe):
                def done(ins, key):
                    ins.then_inc(work_full[slot(key)], 1)

                def norm(name, b):
                    n = NORMS.index(("norm", name, b))
                    if x_before(("norm", name, b)):
                        pe.wait_ge(x_ready, x_before(("norm", name, b)))
                    else:
                        pe.wait_ge(x_loaded[b], 16)
                    key = ("tok", name, b)
                    wait_free(pe, key)
                    for t in range(NT):
                        ins = nc.tensor.transpose(bank(key)[:, t * 128:(t + 1) * 128], xT[:, b, t * 128:(t + 1) * 128],
                                                  ident[:])
                    done(ins, key)
                    for _ in range(FM_TICK):
                        yield
                    key = ("fm", name, b)
                    wait_free(pe, key)
                    pe.wait_ge(xn_ready, NT * (n + 1))
                    for t in range(NT):
                        ins = nc.tensor.transpose(bank(key)[:, t * 128:(t + 1) * 128], xn[:, t, :], ident[:])
                    done(ins, key)
                    yield

                def gv(b):
                    pe.wait_ge(h_ready, h_after("0a", b))
                    for n in range(H // 2):
                        wait_s_bank_free(pe, "G", n, b)
                        for h in (2 * n, 2 * n + 1):
                            ins = nc.tensor.matmul(s_bank("G", n, b)[:, (h % 2) * T:(h % 2 + 1) * T], a0[:, h, :],
                                                   hT0[:, b % H_ROOMS], start=True, stop=True)
                        ins.then_inc(g_full, 1)
                        yield
                    pe.wait_ge(weights_in, 16 * 6)
                    for t in range(NT):
                        for n, key in enumerate((("V by act", t, b), ("V by dve", t, b))):
                            wait_s_bank_free(pe, *key)
                            at = W0_AT["v"][0] + 512 * n
                            nc.tensor.matmul(s_bank(*key), hT0[:, b % H_ROOMS, t * 128:(t + 1) * 128],
                                             w0s[:, at:at + 512], start=True, stop=True).then_inc(v_full, 1)
                            yield

                def attention(layer, b):
                    hpo = HEADS_PER_O[layer]
                    if layer != 0:
                        a = QKVS.index(("qkv", layer, b))
                        vroom = a % H_ROOMS
                    g_base, u_base, o_base = G_BASE[layer, b], U_BASE[layer, b], O_BASE[layer, b]

                    def scores(h):
                        u = u_base + h
                        bk = s_bank("s", u)
                        wait_s_bank_free(pe, "s", u)
                        keys = hTb[:, b % H_ROOMS] if layer == 0 else stacks[:, b % ROOMS, 1, h]
                        qs = gTb[:, b % ROOMS, h] if layer == 0 else stacks[:, b % ROOMS, 0, h]
                        if layer == 0:
                            pe.wait_ge(hb_ready, b + 1)
                            pe.wait_ge(gb_ready, H // 2 * b + h // 2 + 1)
                        for q in range(NT):
                            lhs = qs[:, q * 128:(q + 1) * 128]
                            if layer != 3:
                                ins = nc.tensor.matmul(bk[:, q * T:(q + 1) * T], lhs, keys, start=True, stop=True)
                            else:
                                at = q * 128
                                nc.tensor.matmul(bk[:, at:at + (q + 1) * 128], lhs, keys[:, 0:(q + 1) * 128],
                                                 start=True, stop=False)
                                ins = nc.tensor.matmul(bk[:, at + q * 128:at + (q + 1) * 128], identb[:], mask_qk[:],
                                                       start=False, stop=True)
                        ins.then_inc(s_full, 1)

                    def shift_rows(g):
                        wait_s_bank_free(pe, "mT", g_base + g)
                        pe.wait_ge(m2_ready, g_base + g + 1)
                        dst = s_bank("mT", g_base + g)[:, 0:T // 2].bitcast(BF16)
                        for q in range(NT):
                            ins = nc.tensor.transpose(dst[:, q * 128:(q + 1) * 128], m2[:, (g_base + g) % 2, q, :],
                                                      identb[:])
                        ins.then_inc(mT_full, 1)

                    def scores_t(h):
                        u = u_base + h
                        g, j = g_base + h // GH, h % GH
                        bk = psum[:, ST_BANK + u % 2, :]
                        if u >= 2:
                            pe.wait_ge(pt_ready, u - 1)
                        if layer == 0:
                            pe.wait_ge(g_ready, H // 2 * b + h // 2 + 1)
                        if j == 0:
                            pe.wait_ge(mT_ready, g + 1)
                        if u == 0:
                            pe.wait_ge(more_consts, 1)
                        shift = mT[:, g % 2, :]
                        for k in range(NT):
                            if layer == 0:
                                lhs, rhs = hT0[:, b % H_ROOMS, k * 128:(k + 1) * 128], gT[:, b % ROOMS, h]
                            else:
                                lhs, rhs = stacks[:, b % ROOMS, 1, h, k * 128:(k + 1) * 128], stacks[:, b % ROOMS, 0, h]
                            q0 = k * 128 if layer == 3 else 0
                            at = k * T
                            dst = bk[:, at:at + T - q0]
                            nc.tensor.matmul(dst, lhs, rhs[:, q0:T], start=True, stop=False)
                            if layer == 3:
                                nc.tensor.matmul(bk[:, at:at + 128], identb[:], mask_kq[:], start=False, stop=False)
                            ins = nc.tensor.matmul(dst, sel[:, j, :], shift[:, q0:T], start=False, stop=True)
                        ins.then_inc(st_full, 1)

                    def values(h):
                        u = u_base + h
                        o = o_base + h // hpo
                        bk = psum[:, O_BANK + o % 2, :]
                        m = 128 // hpo
                        at = m * (h % hpo)
                        if h == 0 and layer == 0:
                            pe.wait_ge(v_by_act, NT * (b + 1))
                            pe.wait_ge(v_by_dve, NT * (b + 1))
                        if h == 0 and layer != 0:
                            pe.wait_ge(vpad_ready, NT * (a + 1))
                        if h % hpo == 0 and o >= 2:
                            pe.wait_ge(o_done, o - 1)
                        pe.wait_ge(pt_ready, u + 1)
                        weights = pt[:, u % PT_RING, :]
                        for k in range(NT):
                            lhs = v0[:, b % ROOMS, k, h * DH0:(h + 1) * DH0] if layer == 0 else vpad[:, vroom, k, h, :]
                            q0 = k * 128 if layer == 3 else 0
                            nc.tensor.matmul(bk[at:at + m, q0:T], lhs, weights[:, k * T:(k + 1) * T - q0],
                                             start=(k == 0), stop=(k == NT - 1))
                        q0 = 128 if layer == 3 else 0
                        if q0:
                            nc.tensor.matmul(bk[at:at + m, T:T + q0], ones[:, 0:m], weights[:, 0:q0],
                                             start=True, stop=True)
                        pe.wait_ge(pairsum_ready, u + 1)
                        ins = nc.tensor.matmul(bk[at:at + m, T + q0:2 * T], ones[:, 0:m], pairsum[:, u % 2, q0:T],
                                               start=True, stop=True)
                        ins.then_inc(pt_used, 1)

                    if layer != 0:
                        pe.wait_ge(stack_ready, 16 * 2 * SLOTS * (a + 1))
                    for i in range(STEPS):
                        if i < H:
                            scores(i)
                        yield
                        if mT_step(i) is not None:
                            shift_rows(mT_step(i))
                        if 0 <= i - ST_LAG < H:
                            scores_t(i - ST_LAG)
                        if 0 <= i - PV_LAG < H:
                            values(i - PV_LAG)
                        yield

                def late_mods():
                    cond = col(0, "cond", 0, B)
                    pe.wait_ge(weights_in, 16 * 6)
                    chunks = [(w3s, W3_AT["ada"][0] + D * c, silu[:, 0, :]) for c in range(6)]
                    chunks += [(w2s, W2_AT["gamma"][0], cond), (w2s, W2_AT["beta"][0], cond)]
                    key = ("mods",)
                    wait_free(pe, key)
                    for n, (w, at, c) in enumerate(chunks):
                        ins = nc.tensor.matmul(bank(key)[:, B * n:B * n + B], w[:, at:at + D], c, start=True, stop=True)
                    done(ins, key)
                    key = ("qw",)
                    wait_free(pe, key)
                    for b in range(B):
                        ins = nc.tensor.matmul(bank(key)[0:1, D * b:D * b + D], cond[:, b:b + 1],
                                               w1s[:, W1_AT["self_q"][0]:W1_AT["self_q"][1]], start=True, stop=True)
                    done(ins, key)
                    yield

                def project(layer, b):
                    chunks = H // HEADS_PER_O[layer]
                    key = ("proj", layer, b)
                    wait_free(pe, key)
                    pe.wait_ge(o_done, O_BASE[layer, b] + chunks)
                    if layer != 0:
                        pe.wait_ge(pads_in, 16 * 8)
                    w = (w0s[:, W0_AT["out"][0]:W0_AT["out"][1]].rearrange("p (c n) -> p c n", c=8) if layer == 0
                         else wpad[layer])
                    for c in range(chunks):
                        ins = nc.tensor.matmul(bank(key)[:, 0:T], w[:, c, :], oT[:, b % ROOMS, c, :],
                                               start=(c == 0), stop=(c == chunks - 1))
                    done(ins, key)
                    yield

                def mlp(layer, b):
                    ws, at = (w0s, W0_AT) if layer == 0 else (w3s, W3_AT)
                    pe.wait_ge(h_ready, h_after("0b" if layer == 0 else "3b", b))
                    for n in range(2):
                        key = ("ff", layer, n, b)
                        wait_free(pe, key)
                        for c in range(2):
                            w = at["w1"][0] + (2 * n + c) * 128
                            ins = nc.tensor.matmul(bank(key)[:, c * T:(c + 1) * T], ws[:, w:w + 128], hL[:],
                                                   start=True, stop=True)
                        done(ins, key)
                    for _ in range(Y_TICK):
                        yield
                    key = ("y", layer, b)
                    wait_free(pe, key)
                    for c in range(FC):
                        pe.wait_ge(ff_ready, FC * MLPS.index(("mlp", layer, b)) + c + 1)
                        ins = nc.tensor.matmul(bank(key)[:, 0:T], ws[:, at["w2"][0] + c * 128:at["w2"][0] + (c + 1) * 128],
                                               ff[:, c, :], start=(c == 0), stop=(c == FC - 1))
                    done(ins, key)
                    yield

                def layer1(b):
                    first = L1_UNITS * b
                    def w1(name, d=0):
                        at = W1_AT[name][0] + d * D
                        return w1s[:, at:at + D]

                    pe.wait_ge(x_ready, x_after("mlp", 0, b))
                    wait_free(pe, ("nz", b))
                    done(nc.tensor.matmul(bank(("nz", b))[0:1, 0:T], ones[:, 0:1], xT[:, b], start=True, stop=True),
                         ("nz", b))
                    yield
                    yield
                    key = ("sf", b)
                    wait_free(pe, key)
                    nc.tensor.matmul(bank(key)[:, 0:T], w1("self_v"), xT[:, b], start=True, stop=False)
                    pe.wait_ge(nz_ready, b + 1)
                    done(nc.tensor.matmul(bank(key)[:, 0:T], qw_all[:, b, :], nz[:], start=False, stop=True), key)
                    yield
                    yield
                    pe.wait_ge(sf_ready, b + 1)
                    key = ("q1", b)
                    wait_free(pe, key)
                    for d in range(2):
                        ins = nc.tensor.matmul(bank(key)[:, d * T:(d + 1) * T], w1("q", d), sfT[:],
                                               start=True, stop=True)
                    done(ins, key)
                    key = ("k1", b)
                    wait_free(pe, key)
                    for d in range(2):
                        ins = nc.tensor.matmul(bank(key)[:, d * NG:(d + 1) * NG], w1("k", d), sfT[:, 0:NG],
                                               start=True, stop=True)
                    done(ins, key)
                    yield
                    key = ("v1", b)
                    wait_free(pe, key)
                    pe.wait_ge(sfrep_ready, 2 * b + 1)
                    for d in range(2):
                        ins = nc.tensor.matmul(bank(key)[:, d * D:(d + 1) * D], sfrep[:].rearrange("p h m -> p (h m)"),
                                               w1("out", d), start=True, stop=True)
                    done(ins, key)
                    yield
                    yield
                    for i in range(L1_UNITS + L1_LAG):
                        w = i - L1_Y
                        if 0 <= w < L1_UNITS:
                            key, d = ("y1", w, b), w % 2
                            wait_free(pe, key)
                            pe.wait_ge(wT_ready, first + w + 1)
                            if w == 0:
                                pe.wait_ge(vbd_ready, 2 * (b + 1))
                            for c in range(4):
                                ins = nc.tensor.matmul(bank(key)[:, 0:128], vbd[:, d, c, :],
                                                       wT[:, w % 2, c * 128:(c + 1) * 128],
                                                       start=(c == 0), stop=(c == 3))
                            done(ins, key)
                        if i < L1_UNITS:
                            t, d = i // 2, i % 2
                            key = ("s1", i, b)
                            wait_free(pe, key)
                            if i == 0:
                                pe.wait_ge(q1_ready, 2 * (b + 1))
                                pe.wait_ge(kbd_ready, 2 * (b + 1))
                            done(nc.tensor.matmul(bank(key)[:, 0:H * NG], q1T[:, d, t * 128:(t + 1) * 128],
                                                  kbd[:, d], start=True, stop=True), key)
                        w = i - L1_TURN
                        if 0 <= w < L1_UNITS:
                            key = ("wT", w, b)
                            wait_free(pe, key)
                            pe.wait_ge(wgt_ready, first + w + 1)
                            for c in range(4):
                                ins = nc.tensor.transpose(bank(key)[:, c * 128:(c + 1) * 128],
                                                          wgt[:, w % 2, 4 * c:4 * c + 4, :].rearrange(
                                                              "p h m -> p (h m)"), ident[:])
                            done(ins, key)
                        yield

                def qkv(layer, b):
                    ws, at = (w2s, W2_AT) if layer == 2 else (w3s, W3_AT)
                    pe.wait_ge(h_ready, h_after(f"{layer}a", b))
                    key = ("qk", layer, b)
                    wait_free(pe, key)
                    for s, name in enumerate("qk"):
                        ins = nc.tensor.matmul(bank(key)[:, s * T:(s + 1) * T], ws[:, at[name][0]:at[name][1]], hL[:],
                                               start=True, stop=True)
                    done(ins, key)
                    key = ("v", layer, b)
                    wait_free(pe, key)
                    for t in range(NT):
                        ins = nc.tensor.matmul(bank(key)[:, t * D:(t + 1) * D], hL[:, t * 128:(t + 1) * 128],
                                               ws[:, at["v"][0]:at["v"][1]], start=True, stop=True)
                    done(ins, key)
                    yield

                walk({"late mods": late_mods} | dict(norm=norm, gv=gv, attention=attention, project=project, mlp=mlp,
                                                      layer1=layer1, qkv=qkv))



def kernel(**inputs):
    import numpy as np
    import concourse.bacc as bacc
    from concourse.bass_utils import run_bass_kernel_spmd

    a = {k: np.asarray(v) for k, v in inputs.items()}

    def pack(*blocks):
        return np.ascontiguousarray(np.concatenate(blocks, axis=1))

    def heads_out(w):
        c = w.shape[0] // 128
        return w.reshape(c, 128, w.shape[1]).transpose(1, 0, 2).reshape(128, c * w.shape[1])

    def vcols(*vectors):
        return [v.reshape(-1, 128).T for v in vectors]

    qkv0 = a["L0_cond_W_qkv"]
    hd = H * DH0
    wqk0 = np.stack([qkv0[:, 0:hd].T.reshape(H, DH0, D), qkv0[:, hd:2 * hd].T.reshape(H, DH0, D)])
    w2qkv = a["L2_cond_Wqkv"].reshape(D, 3, D)
    b2qkv = a["L2_cond_bqkv"].reshape(D, 3)
    self_t = a["L1_cond_W_self"].T
    mod2 = pack(*vcols(a["L0_cond_b_mod"], a["L3_cond_bada"], a["L2_cond_bg"], a["L2_cond_bb"]))
    arrays = {
        "x_t": a["x"].transpose(0, 2, 1),
        "adj": a["mask_BxSxSx11_ik0"],
        "w0": pack(a["L0_cond_W_mod"], qkv0[:, 2 * hd:], heads_out(a["L0_cond_W_out"]), a["L0_cond_W1"],
                   heads_out(a["L0_cond_W2"])),
        "wqk0": wqk0.transpose(2, 0, 1, 3),
        "w1": pack(self_t[0:D], self_t[D:], *[a["L1_cond_Wq"][d].T for d in range(2)],
                   *[a["L1_cond_Wk"][d].T for d in range(2)],
                   *[a["L1_cond_Wout"][d].reshape(D, D).T for d in range(2)]),
        "w2": pack(a["L2_cond_Wg"].T, a["L2_cond_Wb"].T, *[w2qkv[:, c].T for c in range(3)]),
        "w3": pack(a["L3_cond_Wqkv"], a["L3_cond_W1"], heads_out(a["L3_cond_W2"]), a["L3_cond_Wada"]),
        "wp2": a["L2_cond_Wp"].T,
        "wproj3": a["L3_cond_Wproj"],
        "vecs": pack(mod2, *vcols(
            a["L0_cond_b_out"], a["L0_cond_b2"], a["L0_cond_b1"], a["L1_cond_b_self"], a["L1_cond_bq"], a["L1_cond_bk"],
            a["L1_cond_bout"], a["L2_cond_ln_g"], a["L2_cond_ln_b"], b2qkv[:, 0], b2qkv[:, 1], a["L2_cond_bp"],
            a["L3_cond_bproj"], a["L3_cond_b2"], a["L3_cond_b1"], a["L3_cond_g1"], a["L3_cond_be1"], a["L3_cond_g2"],
            a["L3_cond_be2"], a["cond_1024"])),
        "rows": np.concatenate([b2qkv[:, 2], a["L1_cond_w_bias"], a["L1_cond_b_bias"].reshape(1)]).reshape(1, -1),
    }
    nc = bacc.Bacc("TRN2", target_bir_lowering=False, num_devices=1)
    args = {}
    for name, v in arrays.items():
        arrays[name] = v = np.ascontiguousarray(v)
        args[name] = nc.dram_tensor(name, v.shape, mybir.dt.from_np(v.dtype), kind="ExternalInput").ap()
    out_t = nc.dram_tensor("out_t", (B, D, T), F32, kind="ExternalOutput").ap()
    cond_seq_kernel(nc, out_t=out_t, **args)
    r = run_bass_kernel_spmd(nc, [arrays], core_ids=[0])
    return np.ascontiguousarray(r.results[0]["out_t"].transpose(0, 2, 1))
```
